# Optimizing a Trainium2 kernel written in Bass

```python
import numpy as np
import jax
import jax.numpy as jnp

def _softmax(x, axis=-1):
    return jax.nn.softmax(x, axis=axis)

def _gelu(x):
    return jax.nn.gelu(x, approximate=True)

def _silu(x):
    return jax.nn.silu(x)

def _sigmoid(x):
    return jax.nn.sigmoid(x)

def _layernorm(x, axis=-1, eps=1e-05):
    m = jnp.mean(x, axis=axis, keepdims=True)
    v = jnp.var(x, axis=axis, keepdims=True)
    return (x - m) / jnp.sqrt(v + eps)

def _scatter_add(tgt, idx, src, axis=0):
    return tgt.at[idx].add(src)

def _segment_sum(src, seg, n):
    return jax.ops.segment_sum(src, seg, n)
kernel_name = 'mk_macaron_d1_jaxref_r8_1938ff'

def setup_inputs(seed: int=0):
    np.random.seed(seed)
    _w = jnp.asarray

    def _L0_attn_setup():
        import jax, jax.numpy as jnp
        import numpy as np
        HIDDEN = 512
        NH = 32
        NKV = 8
        HD = 128
        GS = 128
        BASE = 10000.0
        B, S = (2, 256)

        def _dequant(codes, scales):
            w = codes.astype(jnp.float32) - 8.0
            return w * jnp.repeat(scales, GS, axis=0)

        def _rope(x):
            s, d = (x.shape[2], x.shape[3])
            pos = jnp.arange(s, dtype=jnp.float32)
            inv_freq = 1.0 / BASE ** (jnp.arange(0, d, 2, dtype=jnp.float32) / d)
            f = pos[:, None] * inv_freq[None, :]
            cos = jnp.cos(f)[None, None]
            sin = jnp.sin(f)[None, None]
            xe = x[..., ::2]
            xo = x[..., 1::2]
            re = xe * cos - xo * sin
            ro = xo * cos + xe * sin
            return jnp.stack([re, ro], axis=-1).reshape(x.shape)
        key = jax.random.key(seed)
        ks = jax.random.split(key, 9)

        def codes(k, i, o):
            return jax.random.randint(k, (i, o), 0, 16, dtype=jnp.int32)

        def scales(k, i, o):
            return jax.random.uniform(k, (i // GS, o), dtype=jnp.float32) * 0.02
        return {'hidden_states': jax.random.normal(ks[0], (B, S, HIDDEN), jnp.float32), 'q_codes': codes(ks[1], HIDDEN, NH * HD), 'q_scales': scales(ks[2], HIDDEN, NH * HD), 'k_codes': codes(ks[3], HIDDEN, NKV * HD), 'k_scales': scales(ks[4], HIDDEN, NKV * HD), 'v_codes': codes(ks[5], HIDDEN, NKV * HD), 'v_scales': scales(ks[6], HIDDEN, NKV * HD), 'o_codes': codes(ks[7], NH * HD, HIDDEN), 'o_scales': scales(ks[8], NH * HD, HIDDEN)}
    _L0_attn_in = _L0_attn_setup()

    def _L0_ffn_setup():
        import jax, jax.numpy as jnp
        import numpy as np
        N_EXPERTS = 28
        TOP_K = 2
        RANK = 8
        LORA_ALPHA = 16
        SCALING = LORA_ALPHA / RANK
        TEMP = 1.0
        key = jax.random.key(seed)
        ks = jax.random.split(key, 5)
        B, S, D_IN, D_OUT = (4, 256, 512, 512)
        x = jax.random.normal(ks[0], (B, S, D_IN), dtype=jnp.float32)
        base_W = jax.random.normal(ks[1], (D_OUT, D_IN), dtype=jnp.float32) * (1.0 / np.sqrt(D_IN))
        gate_W = jax.random.normal(ks[2], (N_EXPERTS, D_IN), dtype=jnp.float32) * (1.0 / np.sqrt(D_IN))
        lora_A = jax.random.normal(ks[3], (N_EXPERTS, RANK, D_IN), dtype=jnp.float32) * (1.0 / np.sqrt(D_IN))
        lora_B = jax.random.normal(ks[4], (N_EXPERTS, D_OUT, RANK), dtype=jnp.float32) * 0.01
        return {'x': x, 'base_W': base_W, 'gate_W': gate_W, 'lora_A': lora_A, 'lora_B': lora_B}
    _L0_ffn_in = _L0_ffn_setup()
    _d = {'L0_attn_hidden_states': _L0_attn_in['hidden_states'], 'L0_attn_q_codes': _L0_attn_in['q_codes'], 'L0_attn_q_scales': _L0_attn_in['q_scales'], 'L0_attn_k_codes': _L0_attn_in['k_codes'], 'L0_attn_k_scales': _L0_attn_in['k_scales'], 'L0_attn_v_codes': _L0_attn_in['v_codes'], 'L0_attn_v_scales': _L0_attn_in['v_scales'], 'L0_attn_o_codes': _L0_attn_in['o_codes'], 'L0_attn_o_scales': _L0_attn_in['o_scales'], 'L0_ffn_base_W': _L0_ffn_in['base_W'], 'L0_ffn_gate_W': _L0_ffn_in['gate_W'], 'L0_ffn_lora_A': _L0_ffn_in['lora_A'], 'L0_ffn_lora_B': _L0_ffn_in['lora_B']}
    _x0 = _d['L0_attn_hidden_states']
    _d['L0_attn_hidden_states'] = jax.random.normal(jax.random.fold_in(jax.random.key(seed), 1), (8, 256, 512), dtype=_x0.dtype)
    del _x0
    return _d

def reference(L0_attn_hidden_states, L0_attn_q_codes, L0_attn_q_scales, L0_attn_k_codes, L0_attn_k_scales, L0_attn_v_codes, L0_attn_v_scales, L0_attn_o_codes, L0_attn_o_scales, L0_ffn_base_W, L0_ffn_gate_W, L0_ffn_lora_A, L0_ffn_lora_B):

    def _L0_attn_ref(hidden_states, q_codes, q_scales, k_codes, k_scales, v_codes, v_scales, o_codes, o_scales):
        import jax, jax.numpy as jnp
        import numpy as np
        HIDDEN = 512
        NH = 32
        NKV = 8
        HD = 128
        GS = 128
        BASE = 10000.0
        B, S = (2, 256)

        def _dequant(codes, scales):
            w = codes.astype(jnp.float32) - 8.0
            return w * jnp.repeat(scales, GS, axis=0)

        def _rope(x):
            s, d = (x.shape[2], x.shape[3])
            pos = jnp.arange(s, dtype=jnp.float32)
            inv_freq = 1.0 / BASE ** (jnp.arange(0, d, 2, dtype=jnp.float32) / d)
            f = pos[:, None] * inv_freq[None, :]
            cos = jnp.cos(f)[None, None]
            sin = jnp.sin(f)[None, None]
            xe = x[..., ::2]
            xo = x[..., 1::2]
            re = xe * cos - xo * sin
            ro = xo * cos + xe * sin
            return jnp.stack([re, ro], axis=-1).reshape(x.shape)
        b, s, _ = hidden_states.shape
        q = hidden_states @ _dequant(q_codes, q_scales)
        k = hidden_states @ _dequant(k_codes, k_scales)
        v = hidden_states @ _dequant(v_codes, v_scales)
        q = q.reshape(b, s, NH, HD).transpose(0, 2, 1, 3)
        k = k.reshape(b, s, NKV, HD).transpose(0, 2, 1, 3)
        v = v.reshape(b, s, NKV, HD).transpose(0, 2, 1, 3)
        q = _rope(q)
        k = _rope(k)
        rf = NH // NKV
        k = jnp.repeat(k, rf, axis=1)
        v = jnp.repeat(v, rf, axis=1)
        scale = HD ** (-0.5)
        causal = jnp.tril(jnp.ones((s, s), dtype=bool))
        mask = jnp.where(causal, 0.0, -jnp.inf).astype(q.dtype)
        scores = jnp.einsum('bhqd,bhkd->bhqk', q, k) * scale + mask[None, None]
        attn = jax.nn.softmax(scores, axis=-1)
        out = jnp.einsum('bhqk,bhkd->bhqd', attn, v)
        out = out.transpose(0, 2, 1, 3).reshape(b, s, NH * HD)
        return out @ _dequant(o_codes, o_scales)

    def _L0_ffn_ref(x, base_W, gate_W, lora_A, lora_B):
        import jax, jax.numpy as jnp
        import numpy as np
        N_EXPERTS = 28
        TOP_K = 2
        RANK = 8
        LORA_ALPHA = 16
        SCALING = LORA_ALPHA / RANK
        TEMP = 1.0
        B, S, D_in = x.shape
        xf = x.reshape(B * S, D_in)
        base = xf @ base_W.T
        logits = xf @ gate_W.T
        top_vals, top_idx = jax.lax.top_k(logits, TOP_K)
        top_probs = jax.nn.softmax(top_vals / TEMP, axis=-1)
        N = xf.shape[0]
        gate_full = jnp.zeros((N, N_EXPERTS), dtype=xf.dtype).at[jnp.arange(N)[:, None], top_idx].add(top_probs)
        h = jnp.einsum('nd,erd->ner', xf, lora_A)
        h = h * (gate_full * SCALING)[:, :, None]
        lora_out = jnp.einsum('ner,eor->no', h, lora_B)
        out = base + lora_out
        return out.reshape(B, S, -1)
    x = L0_attn_hidden_states
    x = x + 0.5 * _L0_ffn_ref(_layernorm(x, axis=-1), L0_ffn_base_W, L0_ffn_gate_W, L0_ffn_lora_A, L0_ffn_lora_B)
    x = x + _L0_attn_ref(_layernorm(x, axis=-1), L0_attn_q_codes, L0_attn_q_scales, L0_attn_k_codes, L0_attn_k_scales, L0_attn_v_codes, L0_attn_v_scales, L0_attn_o_codes, L0_attn_o_scales)
    x = x + 0.5 * _L0_ffn_ref(_layernorm(x, axis=-1), L0_ffn_base_W, L0_ffn_gate_W, L0_ffn_lora_A, L0_ffn_lora_B)
    return x

_drawn_inputs = setup_inputs


def setup_inputs(seed=0):
    import zlib

    import numpy as np

    out = dict(_drawn_inputs(seed))
    spreads = {}
    factors = {}
    for name, (base, spread) in spreads.items():
        noise = np.random.default_rng([zlib.crc32(name.encode()), seed]).standard_normal(out[name].shape)
        drawn = base * np.exp(spread * noise) if base else spread * noise
        out[name] = jnp.asarray(drawn.astype(out[name].dtype))
    for name, factor in factors.items():
        out[name] = (out[name] * factor).astype(out[name].dtype)
    return out
```

```python
from contextlib import ExitStack

import numpy as np

import concourse.bass as bass
from concourse import mybir

F32 = mybir.dt.float32
F32R = mybir.dt.float32r
BF16 = mybir.dt.bfloat16
I32 = mybir.dt.int32
U32 = mybir.dt.uint32
ALU = mybir.AluOpType
ACT = mybir.ActivationFunctionType
AX = mybir.AxisListType

P = 128
B, S, D = 8, 256, 512
TILES = B * S // P
HALVES = S // P
DC = D // P
NH, NKV, HD = 32, 8, 128
REP = NH // NKV
QW = REP * HD
CW = QW + 2 * HD
GW = DC * CW + REP * D
ITEMS = NKV * B
PIECES = B
PW = GW // PIECES
E, R = 28, 8
ER = E * R
EW = E + ER
KC = ER // 2
FW = DC * (D + EW) + 2 * D
FPIECES = -(-FW // PW)
EPS = 1e-5
FLOOP = (TILES - 6) // 2
assert FLOOP + 3 == PIECES and FPIECES <= B - 1
AHEAD = B + 1
Q_AT = [c * CW for c in range(DC)]
KV_AT = [c * CW + QW for c in range(DC)]
O_AT = [DC * CW + h * D for h in range(REP)]
F_BASE = [c * (D + EW) for c in range(DC)]
F_GATE = [c * (D + EW) + D for c in range(DC)]
F_LORA = [DC * (D + EW) + c * D for c in range(2)]


def build(nc, x_in, w_codes, w_scales, f_weights, cos_q, sin_q, cos_k, sin_k, mask_in, ident_in,
          ident16_in, iota_in, out):
    with ExitStack() as ctx:
        def sb(name, shape, dt=F32):
            return ctx.enter_context(nc.sbuf_tensor(name, shape, dt))

        def psum(name, banks=1):
            return ctx.enter_context(nc.psum_tensor(name, [P, banks * 512], F32))

        def sem(name):
            return ctx.enter_context(nc.semaphore(name))

        x = sb("x", [P, TILES * D])
        xT = sb("xT", [P, B * DC * S])
        w_hi = sb("w_hi", [P, 2 * GW], F32R)
        w_lo = sb("w_lo", [P, 2 * GW], F32R)
        codes = sb("codes", [P, 2 * PW], I32)
        scales = sb("scales", [P, 2 * PW])
        xs_hi = sb("xs_hi", [P, DC, S], F32R)
        xs_lo = sb("xs_lo", [P, DC, S], F32R)
        probs = sb("probs", [P, 3 * 512])
        pT_hi = sb("pT_hi", [P, 3, 512], F32R)
        pT_lo = sb("pT_lo", [P, 3, 512], F32R)
        oT_hi = sb("oT_hi", [P, HALVES, 512], F32R)
        oT_lo = sb("oT_lo", [P, HALVES, 512], F32R)
        qT0 = sb("qT0", [P, 512])
        qT1_hi = sb("qT1_hi", [P, 512], F32R)
        qT1_lo = sb("qT1_lo", [P, 512], F32R)
        kT = sb("kT", [P, P])
        kT_hi = sb("kT_hi", [P, S], F32R)
        kT_lo = sb("kT_lo", [P, S], F32R)
        v_hi = sb("v_hi", [P, HALVES, HD], F32R)
        v_lo = sb("v_lo", [P, HALVES, HD], F32R)
        rope_c = sb("rope_c", [P, HALVES, QW])
        rope_s = sb("rope_s", [P, HALVES, QW])
        ropek_c = sb("ropek_c", [P, HALVES, HD])
        ropek_s = sb("ropek_s", [P, HALVES, HD])
        nmax = sb("nmax", [P, HALVES, REP])
        rsum = sb("rsum", [P, HALVES, REP])
        rinv = sb("rinv", [P, HALVES, REP])
        cosq = sb("cosq", [P, HALVES, 64])
        sinq = sb("sinq", [P, HALVES, 2, 64])
        cosk = sb("cosk", [P, HALVES, 64])
        sink = sb("sink", [P, HALVES, 2, 64])
        mask = sb("mask", [P, 4 * P], BF16)
        ident = sb("ident", [P, P])
        ident16 = sb("ident16", [P, P], BF16)
        iota = sb("iota", [P, E])
        bn = sb("bn", [P, 6])
        mv1 = sb("mv1", [P, 2])
        mv = sb("mv", [P, TILES, 2])
        ln_v = sb("ln_v", [P, TILES])
        ln_s = sb("ln_s", [P, TILES])
        ln_t = sb("ln_t", [P, TILES])
        rstd = sb("rstd", [P, TILES])
        logits = sb("logits", [P, E])
        top = sb("top", [P, 8])
        topi = sb("topi", [P, 8], U32)
        topf = sb("topf", [P, 2])
        gap = sb("gap", [P, 1])
        egap = sb("egap", [P, 1])
        den = sb("den", [P, 1])
        pr = sb("pr", [P, 2])
        g1 = sb("g1", [P, E])
        g2 = sb("g2", [P, E])
        gate = sb("gate", [P, E])
        xh = [probs[:, 0:512], probs[:, 512:1024]]
        hg = [rope_c[:, e, 0:ER] for e in range(2)]
        fx_hi = [pT_hi[:, e, :] for e in range(2)]
        fx_lo = [pT_lo[:, e, :] for e in range(2)]
        hT_hi = [oT_hi[0:KC, e, 0:2 * P] for e in range(2)]
        hT_lo = [oT_lo[0:KC, e, 0:2 * P] for e in range(2)]

        q_ps = [psum("q0_ps"), psum("q1_ps")]
        kv_ps = psum("kv_ps")
        s_ps = psum("s_ps", 3)
        y_ps = [psum("y0_ps"), psum("y1_ps")]
        xt_ps = [s_ps[:, 0:512], s_ps[:, 512:1024]]
        ht_ps = [s_ps[:, 1024:1536], kv_ps[:, :]]

        const_in = sem("const_in")
        xin = [sem(f"x_in{k}") for k in range(4)]
        raw_in = sem("raw_in")
        phase_end = sem("phase_end")
        bn_done, mv1_done, mv_done = sem("bn_done"), sem("mv1_done"), sem("mv_done")
        ln_step, ln_root = sem("ln_step"), sem("ln_root")
        xh_done, xt_done, fxh_done, fxl_done = sem("xh_done"), sem("xt_done"), sem("fxh_done"), sem("fxl_done")
        ge_done, hg_done, ht_done, hth_done, htl_done = (sem(n) for n in ("ge_done", "hg_done", "ht_done", "hth_done", "htl_done"))
        ffn_done, upd_done = sem("ffn_done"), sem("upd_done")
        gt = [sem(f"gate_step{k}") for k in range(10)]
        egap_done = sem("egap_done")
        xT_done = sem("xT_done")
        y_out = sem("y_out")
        w_deq, wh_done, wl_done = sem("w_deq"), sem("wh_done"), sem("wl_done")
        s_done = [sem("s0_done"), sem("s1_done")]
        q_done = [sem("q0_done"), sem("q1_done")]
        kv_done = sem("kv_done")
        pt_done = [sem(f"pt{k}_done") for k in range(3)]
        qt_done = [sem("qt0_done"), sem("qt1_done")]
        kt_done = sem("kt_done")
        o_done = [sem("o0_done"), sem("o1_done")]
        y_done = [sem("y0_done"), sem("y1_done")]
        nmax_done = [sem("nmax0_done"), sem("nmax1_done")]
        rinv_done = [sem("rinv0_done"), sem("rinv1_done")]
        mul_done = [sem("mul0_done"), sem("mul1_done")]
        mulk_done = sem("mulk_done")
        vl_done = sem("vl_done")
        ptl_done = [sem(f"ptl{k}_done") for k in range(3)]
        qtl_done, ktl_done = sem("qtl_done"), sem("ktl_done")
        ol_done = [sem("ol0_done"), sem("ol1_done")]
        acc_done = [sem("acc0_done"), sem("acc1_done")]
        exp_done = [sem("exp0_done"), sem("exp1_done")]
        vh_done, xsh_done = sem("vh_done"), sem("xsh_done")
        pth_done = [sem(f"pth{k}_done") for k in range(3)]
        qt0_copied, qth_done, kt_copied, kth_done = sem("qt0_copied"), sem("qth_done"), sem("kt_copied"), sem("kth_done")
        oh_done = [sem("oh0_done"), sem("oh1_done")]
        norm_done = [sem("norm0_done"), sem("norm1_done")]
        rope_done = [sem("rope0_done"), sem("rope1_done")]
        ropek_done = sem("ropek_done")
        xsl_done = sem("xsl_done")

        def need(eng, s, n):
            if not isinstance(n, int) or n > 0:
                eng.wait_ge(s, n)

        def value(eng, v):
            if isinstance(v, int):
                return v
            v = eng.snap(v)
            eng.to_reg(v)
            return v

        def need_apart(eng, s, n):
            n = value(eng, n)
            eng.wait_ge(const_in, 16 * NDMA_CONST)
            need(eng, s, n)

        def barrier(eng, n):
            eng.drain().then_inc(phase_end, 1)
            eng.wait_ge(phase_end, 4 * n)

        W0, F2 = FPIECES, FPIECES + ITEMS
        SLOT1, SLOT0 = GW, 0
        NDMA_CONST = 8

        def f32(ap):
            return ap.bitcast(F32)

        block = ctx.enter_context(nc.Block())

        @block.sync
        def _(sp):
            for dst, src in ((cosq, cos_q), (sinq, sin_q), (cosk, cos_k), (sink, sin_k), (mask, mask_in),
                             (ident, ident_in), (ident16, ident16_in), (iota, iota_in)):
                sp.dma_start(dst[:], src).then_inc(const_in, 16)
            n = TILES // 4
            for k in range(4):
                sp.dma_start(x[:, k * n * D:(k + 1) * n * D].rearrange("p (t d) -> p t d", t=n),
                             x_in.rearrange("(t p) d -> p t d", p=P)[:, k * n:(k + 1) * n, :]).then_inc(xin[k], 16)

            def room(r):
                at = value(sp, (r & 1) * PW)
                before, ins = value(sp, r - 1), value(sp, 32 * r)
                need_apart(sp, wl_done, before)
                need(sp, raw_in, ins)
                return at

            def ffn_piece(r, f):
                at = room(r)
                sp.dma_start(codes[:, bass.ds(at, PW)].bitcast(F32),
                             f_weights[bass.ds(f, 1)].rearrange("a p n -> (a p) n")).then_inc(raw_in, 32)

            def group_piece(r, p):
                at = room(r)
                sp.dma_start(codes[:, bass.ds(at, PW)],
                             w_codes[bass.ds(p, 1)].rearrange("a p n -> (a p) n")).then_inc(raw_in, 16)
                sp.dma_start(scales[:, bass.ds(at, PW)],
                             w_scales[bass.ds(p, 1), :].to_broadcast([P, PW])).then_inc(raw_in, 16)

            for f in range(FPIECES):
                ffn_piece(f, f)
            with sp.Fori(0, ITEMS) as p:
                group_piece(p + W0, p)
            with sp.Fori(0, FPIECES) as f:
                ffn_piece(f + F2, f)
            with sp.Fori(0, TILES) as t:
                need_apart(sp, upd_done, t + (TILES + 1))
                sp.dma_start(out[bass.ds(t * P, P), :], x[:, bass.ds(t * D, D)]).then_inc(y_out, 16)
            sp.wait_ge(y_out, 16 * TILES)

        @block.tensor
        def _(pe):
            def split_product(ps, stationary, moving, first, last):
                (a_hi, a_lo), (b_hi, b_lo) = stationary, moving
                pe.matmul(ps, a_hi, b_hi, start=first, stop=False, skip_group_check=True)
                pe.matmul(ps, a_lo, b_hi, start=False, stop=False, skip_group_check=True)
                return pe.matmul(ps, a_hi, b_lo, start=False, stop=last, skip_group_check=True)

            def x_transpose(n, e, before):
                pe.wait_ge(xh_done, n + (before + 1))
                need(pe, fxl_done, n - 1)
                for c in range(DC):
                    mm = pe.transpose(xt_ps[e][:, c * P:(c + 1) * P], xh[e][:, c * P:(c + 1) * P], ident[:, :])
                mm.then_inc(xt_done, 1)

            def ffn_in(n, e, slot):
                def moving(at, w):
                    return w_hi[:, slot + at:slot + at + w], w_lo[:, slot + at:slot + at + w]

                pe.wait_ge(fxl_done, n + 1)
                need(pe, hg_done, n - 1)
                for c in range(DC):
                    st = [t[e][:, c * P:(c + 1) * P] for t in (fx_hi, fx_lo)]
                    mm = split_product(q_ps[e][:, 0:EW], st, moving(F_GATE[c], EW), c == 0, c == DC - 1)
                mm.then_inc(ge_done, 1)

            def ffn_base(n, e, slot):
                need(pe, upd_done, n - 1)
                for c in range(DC):
                    st = [t[e][:, c * P:(c + 1) * P] for t in (fx_hi, fx_lo)]
                    mv_ = [w[:, slot + F_BASE[c]:slot + F_BASE[c] + D] for w in (w_hi, w_lo)]
                    split_product(y_ps[e][:, :], st, mv_, c == 0, False)

            def h_transpose(n, e):
                pe.wait_ge(hg_done, n + 1)
                need(pe, htl_done, n - 1)
                for c in range(2):
                    mm = pe.transpose(ht_ps[e][0:KC, c * P:(c + 1) * P], hg[e][:, c * KC:(c + 1) * KC], ident[:, :])
                mm.then_inc(ht_done, 1)

            def ffn_lora(n, e, slot):
                pe.wait_ge(htl_done, n + 1)
                for c in range(2):
                    st = [t[e][:, c * P:(c + 1) * P] for t in (hT_hi, hT_lo)]
                    mv_ = [w[0:KC, slot + F_LORA[c]:slot + F_LORA[c] + D] for w in (w_hi, w_lo)]
                    mm = split_product(y_ps[e][:, :], st, mv_, False, c == 1)
                mm.then_inc(ffn_done, 1)

            def ffn_step(base, t, e, slot, prev=True, here=True, ahead=True):
                n = value(pe, t + base)
                if ahead:
                    x_transpose(n + 1, 1 - e, base)
                if here:
                    ffn_in(n, e, slot)
                if prev:
                    h_transpose(n - 1, 1 - e)
                if here:
                    ffn_base(n, e, slot)
                if prev:
                    ffn_lora(n - 1, 1 - e, slot)

            def ffn(phase, slot):
                base = phase * TILES
                x_transpose(base, 0, base)
                ffn_step(base, 0, 0, slot, prev=False)
                for t in (1, 2):
                    ffn_step(base, t, t % 2, slot)
                with pe.Fori(0, FLOOP) as k:
                    for e in (1, 0):
                        ffn_step(base, 2 * k + (4 - e), e, slot)
                for t in range(TILES - 3, TILES):
                    ffn_step(base, t, t % 2, slot, ahead=t < TILES - 1)
                ffn_step(base, TILES, 0, slot, here=False, ahead=False)

            pe.wait_ge(const_in, 16 * NDMA_CONST)
            pe.wait_ge(wl_done, FPIECES)
            ffn(0, SLOT1)
            barrier(pe, 1)

            def x_transpose_all(t, e):
                pe.wait_ge(xh_done, t + (TILES + 1))
                need(pe, xT_done, t - 1)
                for c in range(DC):
                    mm = pe.transpose(xt_ps[e][:, c * P:(c + 1) * P], xh[e][:, c * P:(c + 1) * P], ident[:, :])
                mm.then_inc(xt_done, 1)

            for e in range(2):
                x_transpose_all(e, e)
            with pe.Fori(1, TILES // 2) as k:
                for e in range(2):
                    x_transpose_all(2 * k + e, e)
            barrier(pe, 2)

            def scores(i):
                n = value(pe, i + 1)
                pe.wait_ge(qt0_copied, n)
                pe.wait_ge(kt_copied, n)
                need(pe, ptl_done[0], i)
                pe.matmul(s_ps[:, 0:512], ident16[:, :], mask[:, :], start=True, stop=False, skip_group_check=True)
                for h in range(REP):
                    mm = pe.matmul(s_ps[:, h * P:(h + 1) * P], qT0[:, h * P:(h + 1) * P], kT[:, :],
                                   start=False, stop=h == REP - 1, skip_group_check=True)
                mm.then_inc(s_done[0], 1)
                pe.wait_ge(qtl_done, n)
                pe.wait_ge(ktl_done, n)
                need(pe, ptl_done[1], i)
                need(pe, ptl_done[2], i)
                for h2 in range(REP // 2):
                    bank = s_ps[:, 512 * (1 + h2):512 * (2 + h2)].rearrange("p (h k) -> p h k", h=2)
                    pe.matmul(bank[:, :, P:S], ident16[:, :], mask[:, 0:2 * P].rearrange("p (h k) -> p h k", h=2),
                              start=True, stop=False, skip_group_check=True)
                    for h in range(2):
                        q = (2 * h2 + h) * P
                        mm = split_product(bank[:, h, :], (qT1_hi[:, q:q + P], qT1_lo[:, q:q + P]),
                                           (kT_hi[:, :], kT_lo[:, :]), False, h == 1)
                mm.then_inc(s_done[1], 1)

            def project(j):
                pe.wait_ge(xsl_done, j + 1)
                pe.wait_ge(wl_done, (j >> 3 << 3) + (W0 + PIECES) if not isinstance(j, int) else W0 + PIECES * (j // B + 1))
                slot = value(pe, ((j >> 3) & 1) * GW)
                for t in range(HALVES):
                    need(pe, (qt0_copied, qtl_done)[t], j)
                    for c in range(DC):
                        at = value(pe, slot + Q_AT[c])
                        mm = split_product(q_ps[t][:, :], [v[:, c, t * P:(t + 1) * P] for v in (xs_hi, xs_lo)],
                                           [w[:, bass.ds(at, QW)] for w in (w_hi, w_lo)], c == 0, c == DC - 1)
                    mm.then_inc(q_done[t], 1)
                    if t == 0:
                        need(pe, ktl_done, j)
                        need(pe, vl_done, j)
                    for c in range(DC):
                        at = value(pe, slot + KV_AT[c])
                        mm = split_product(kv_ps[:, t * S:(t + 1) * S],
                                           [v[:, c, t * P:(t + 1) * P] for v in (xs_hi, xs_lo)],
                                           [w[:, bass.ds(at, S)] for w in (w_hi, w_lo)], c == 0, c == DC - 1)
                mm.then_inc(kv_done, 1)

            def qk_transpose(j):
                n = value(pe, j + 1)
                for t in range(HALVES):
                    pe.wait_ge(rope_done[t], n)
                    for h in range(REP):
                        mm = pe.transpose(q_ps[t][:, h * P:(h + 1) * P], rope_c[:, t, h * P:(h + 1) * P], ident[:, :])
                    mm.then_inc(qt_done[t], 1)
                    if t == 0:
                        pe.wait_ge(ropek_done, n)
                        for u in range(HALVES):
                            mm = pe.transpose(kv_ps[:, u * S:u * S + P], ropek_c[:, u, :], ident[:, :])
                        mm.then_inc(kt_done, 1)

            def p_transpose(i):
                n = value(pe, i + 1)
                pe.wait_ge(norm_done[0], n)
                for h in range(REP):
                    mm = pe.transpose(s_ps[:, h * P:(h + 1) * P], probs[:, h * P:(h + 1) * P], ident[:, :])
                mm.then_inc(pt_done[0], 1)
                pe.wait_ge(norm_done[1], n)
                for kc in range(HALVES):
                    for h in range(REP):
                        at = 512 + h * S + kc * P
                        to = 512 * (1 + kc) + h * P
                        mm = pe.transpose(s_ps[:, to:to + P], probs[:, at:at + P], ident[:, :])
                    mm.then_inc(pt_done[1 + kc], 1)

            def values(i):
                n = value(pe, i + 1)
                pe.wait_ge(vl_done, n)
                for t in range(HALVES):
                    need(pe, acc_done[t], i)
                    for kc in range(t + 1):
                        k = (0 if t == 0 else 1 + kc)
                        pe.wait_ge(ptl_done[k], n)
                        mm = split_product(y_ps[t][:, :], (v_hi[:, kc, :], v_lo[:, kc, :]),
                                           (pT_hi[:, k, :], pT_lo[:, k, :]), kc == 0, kc == t)
                    mm.then_inc(o_done[t], 1)

            def out_project(j, t):
                pe.wait_ge(ol_done[t], j + 1)
                slot = value(pe, ((j >> 3) & 1) * GW)
                for h in range(REP):
                    at = value(pe, slot + O_AT[h])
                    mm = split_product(y_ps[t][:, :], [o[:, t, h * P:(h + 1) * P] for o in (oT_hi, oT_lo)],
                                       [w[:, bass.ds(at, D)] for w in (w_hi, w_lo)], h == 0, h == REP - 1)
                mm.then_inc(y_done[t], 1)

            def item(i, first=False, last=False):
                scores(i)
                if not last:
                    project(i + 1)
                if not first:
                    out_project(i - 1, 0)
                p_transpose(i)
                if not last:
                    qk_transpose(i + 1)
                if not first:
                    out_project(i - 1, 1)
                values(i)

            project(0)
            qk_transpose(0)
            item(0, first=True)
            with pe.Fori(1, ITEMS - 1) as i:
                item(i)
            item(ITEMS - 1, last=True)
            for t in range(HALVES):
                out_project(ITEMS - 1, t)
            barrier(pe, 3)

            pe.wait_ge(wl_done, F2 + FPIECES)
            ffn(1, SLOT0)

        @block.scalar
        def _(act):
            def split_hi(to, src, done):
                act.activation(to, src, ACT.Copy).then_inc(done, 1)

            def root(phase):
                act.wait_ge(ln_step, 6 * phase + 1)
                act.activation(ln_s[:, :], ln_v[:, :], ACT.Sqrt).then_inc(ln_root, 1)

            def weight_hi(r, at, scaled):
                raw = value(act, (r & 1) * PW)
                if scaled:
                    act.wait_ge(w_deq, r - (W0 - 1))
                    src = scales[:, bass.ds(raw, PW)]
                else:
                    act.wait_ge(raw_in, 32 * (r + 1))
                    src = f32(codes[:, bass.ds(raw, PW)])
                split_hi(w_hi[:, bass.ds(at, PW)], src, wh_done)

            def group_hi(p):
                weight_hi(p + W0, value(act, (p & (2 * PIECES - 1)) * PW), True)

            def ffn(phase):
                base = phase * TILES
                xt_base = 2 * base
                act.wait_ge(xt_done, xt_base + 1)
                split_hi(fx_hi[0], xt_ps[0], fxh_done)

                def step(t, e, prev=True, here=True, ahead=True):
                    n = value(act, t + base)
                    if ahead:
                        act.wait_ge(xt_done, t + (xt_base + 2))
                        split_hi(fx_hi[1 - e], xt_ps[1 - e], fxh_done)
                    if prev:
                        act.wait_ge(ht_done, n)
                        split_hi(hT_hi[1 - e], ht_ps[1 - e][0:KC, 0:2 * P], hth_done)
                    if here:
                        act.wait_ge(gt[3], n + 1)
                        act.activation(egap[:, :], gap[:, :], ACT.Exp).then_inc(egap_done, 1)

                step(0, 0, prev=False)
                for t in (1, 2):
                    step(t, t % 2)
                with act.Fori(0, FLOOP) as k:
                    for e in (1, 0):
                        step(2 * k + (4 - e), e)
                    if phase == 0:
                        group_hi(k)
                for t in range(TILES - 3, TILES):
                    step(t, t % 2, ahead=t < TILES - 1)
                    if phase == 0:
                        group_hi(t - (TILES - 3) + FLOOP)
                step(TILES, 0, here=False, ahead=False)

            for f in range(FPIECES):
                weight_hi(f, SLOT1 + f * PW, False)
            root(0)
            ffn(0)
            barrier(act, 1)

            root(1)
            with act.Fori(0, TILES // 2) as k:
                for e in range(2):
                    act.wait_ge(xt_done, 2 * k + (TILES + e + 1))
                    at = value(act, k * (DC * S))
                    to = xT[:, bass.ds(at, DC * S)].rearrange("p (c t) -> p c t", c=DC)[:, :, e * P:(e + 1) * P]
                    act.activation(to, xt_ps[e].rearrange("p (c t) -> p c t", c=DC), ACT.Copy).then_inc(xT_done, 1)
            barrier(act, 2)

            def stage_hi(j):
                need(act, kv_done, j)
                at = value(act, (j & (B - 1)) * (DC * S))
                split_hi(xs_hi[:, :, :].rearrange("p c t -> p (c t)"), xT[:, bass.ds(at, DC * S)], xsh_done)

            def qk_copies(j):
                n = value(act, j + 1)
                act.wait_ge(qt_done[0], n)
                split_hi(qT0[:, :], q_ps[0][:, :], qt0_copied)
                act.wait_ge(kt_done, n)
                split_hi(kT[:, :], kv_ps[:, 0:P], kt_copied)
                split_hi(kT_hi[:, :].rearrange("p (t k) -> p t k", t=HALVES),
                         kv_ps[:, :].rearrange("p (t k) -> p t k", t=HALVES)[:, :, 0:P], kth_done)
                act.wait_ge(qt_done[1], n)
                split_hi(qT1_hi[:, :], q_ps[1][:, :], qth_done)

            def item(i, first=False, last=False, stage=True, prep=True):
                n = value(act, i + 1)
                need(act, o_done[1], i)
                act.wait_ge(ktl_done, n)
                split_hi(v_hi[:, :, :], kv_ps[:, :].rearrange("p (t k) -> p t k", t=HALVES)[:, :, P:S], vh_done)
                for t in range(HALVES):
                    act.wait_ge(nmax_done[t], n)
                    w = P * (t + 1)
                    for h in range(REP):
                        at = 512 * t + h * w
                        mm = act.activation(probs[:, at:at + w], s_ps[:, at:at + w], ACT.Exp,
                                            bias=nmax[:, t, h:h + 1], accum_out=rsum[:, t, h:h + 1])
                    mm.then_inc(exp_done[t], 1)
                if stage:
                    stage_hi(i + 2)
                if prep:
                    group_hi(i + AHEAD)
                for k in range(3):
                    act.wait_ge(pt_done[k], n)
                    split_hi(pT_hi[:, k, :], s_ps[:, k * 512:(k + 1) * 512], pth_done[k])
                if not last:
                    qk_copies(i + 1)
                for t in range(HALVES):
                    act.wait_ge(o_done[t], n)
                    split_hi(oT_hi[:, t, :], y_ps[t][:, :], oh_done[t])

            stage_hi(0)
            group_hi(PIECES)
            stage_hi(1)
            qk_copies(0)
            item(0, first=True)
            with act.Fori(1, ITEMS - AHEAD) as i:
                item(i)
            with act.Fori(ITEMS - AHEAD, ITEMS - 2) as i:
                item(i, prep=False)
                weight_hi(i + (F2 - ITEMS + AHEAD), SLOT0 + (i - (ITEMS - AHEAD)) * PW, False)
            item(ITEMS - 2, stage=False, prep=False)
            item(ITEMS - 1, last=True, stage=False, prep=False)
            barrier(act, 3)

            root(2)
            ffn(1)

        @block.vector
        def _(dve):
            def tile_stats(t, n, updated=0):
                need_apart(dve, mv_done, n)
                need(dve, upd_done, updated)
                dve.bn_stats(bn[:, :], x[:, bass.ds(t * D, D)]).then_inc(bn_done, 1)
                need_apart(dve, bn_done, n + 1)
                dve.bn_aggr(mv1[:, :], bn[:, :]).then_inc(mv1_done, 1)
                need_apart(dve, mv1_done, n + 1)
                dve.tensor_copy(mv[:, bass.ds(t, 1), :].rearrange("p a b -> p (a b)"), mv1[:, :]).then_inc(mv_done, 1)

            def roots(phase, n):
                dve.wait_ge(mv_done, n)
                b = 6 * phase
                dve.tensor_scalar(ln_v[:, :], mv[:, :, 1], EPS, None, ALU.add).then_inc(ln_step, 1)
                dve.wait_ge(ln_root, phase + 1)
                dve.reciprocal(rstd[:, :], ln_s[:, :]).then_inc(ln_step, 1)
                dve.wait_ge(ln_step, b + 2)
                dve.tensor_tensor(ln_t[:, :], rstd[:, :], rstd[:, :], ALU.mult).then_inc(ln_step, 1)
                dve.wait_ge(ln_step, b + 3)
                dve.tensor_tensor(ln_s[:, :], ln_t[:, :], ln_v[:, :], ALU.mult).then_inc(ln_step, 1)
                dve.wait_ge(ln_step, b + 4)
                dve.tensor_scalar(ln_t[:, :], ln_s[:, :], -0.5, 1.5, ALU.mult, ALU.add).then_inc(ln_step, 1)
                dve.wait_ge(ln_step, b + 5)
                dve.tensor_tensor(rstd[:, :], rstd[:, :], ln_t[:, :], ALU.mult).then_inc(ln_step, 1)
                dve.wait_ge(ln_step, b + 6)

            def norm(t, e):
                dve.tensor_scalar(xh[e], x[:, bass.ds(t * D, D)], mv[:, bass.ds(t, 1), 0], rstd[:, bass.ds(t, 1)],
                                  ALU.subtract, ALU.mult).then_inc(xh_done, 1)

            def split_lo(to, src, hi, done):
                dve.tensor_tensor(to, src, f32(hi), ALU.subtract).then_inc(done, 1)

            def dequant(p):
                r = p + W0
                dve.wait_ge(raw_in, 32 * r + 32)
                at = value(dve, (r & 1) * PW)
                dve.scalar_tensor_tensor(out=scales[:, bass.ds(at, PW)], in0=codes[:, bass.ds(at, PW)], scalar=-8.0,
                                         in1=scales[:, bass.ds(at, PW)], op0=ALU.add, op1=ALU.mult)\
                   .then_inc(w_deq, 1)

            def gates(n, e):
                m = value(dve, n + 1)
                dve.wait_ge(ge_done, m)
                dve.tensor_copy(logits[:, :], q_ps[e][:, 0:E]).then_inc(gt[0], 1)
                need_apart(dve, gt[0], m)
                dve.max(top[:, :], logits[:, :]).then_inc(gt[1], 1)
                need_apart(dve, gt[1], m)
                dve.max_index(topi[:, :], top[:, :], logits[:, :]).then_inc(gt[2], 1)
                dve.tensor_tensor(gap[:, :], top[:, 1:2], top[:, 0:1], ALU.subtract).then_inc(gt[3], 1)
                dve.wait_ge(gt[2], m)
                dve.tensor_copy(topf[:, :], topi[:, 0:2]).then_inc(gt[4], 1)
                dve.wait_ge(egap_done, m)
                dve.tensor_scalar(den[:, :], egap[:, :], 0.5, 0.5, ALU.mult, ALU.add).then_inc(gt[5], 1)
                dve.wait_ge(gt[5], m)
                dve.reciprocal(pr[:, 0:1], den[:, :]).then_inc(gt[6], 1)
                dve.wait_ge(gt[6], m)
                dve.tensor_tensor(pr[:, 1:2], pr[:, 0:1], egap[:, :], ALU.mult).then_inc(gt[7], 1)
                dve.wait_ge(gt[4], m)
                dve.tensor_scalar(g1[:, :], iota[:, :], topf[:, 0:1], pr[:, 0:1], ALU.is_equal, ALU.mult)\
                   .then_inc(gt[8], 1)
                dve.wait_ge(gt[7], m)
                dve.tensor_scalar(g2[:, :], iota[:, :], topf[:, 1:2], pr[:, 1:2], ALU.is_equal, ALU.mult)\
                   .then_inc(gt[8], 1)
                dve.wait_ge(gt[8], 2 * m)
                dve.tensor_tensor(gate[:, :], g1[:, :], g2[:, :], ALU.add).then_inc(gt[9], 1)
                dve.wait_ge(gt[9], m)
                dve.tensor_tensor(hg[e].rearrange("p (e r) -> p e r", e=E),
                                  q_ps[e][:, E:EW].rearrange("p (e r) -> p e r", e=E),
                                  gate[:, :].unsqueeze(2).to_broadcast([P, E, R]), ALU.mult).then_inc(hg_done, 1)

            def ffn(phase):
                base = phase * TILES

                def step(t, e, prev=True, here=True, ahead=True, two=True):
                    n = value(dve, t + base)
                    if ahead:
                        dve.wait_ge(fxh_done, n + 2)
                        split_lo(fx_lo[1 - e], xt_ps[1 - e], fx_hi[1 - e], fxl_done)
                    if prev:
                        dve.wait_ge(hth_done, n)
                        split_lo(hT_lo[1 - e], ht_ps[1 - e][0:KC, 0:2 * P], hT_hi[1 - e], htl_done)
                    if two:
                        norm(t + 2, e)
                    if here:
                        gates(n, e)
                    if prev:
                        dve.wait_ge(ffn_done, n)
                        at = value(dve, (t - 1) * D)
                        xt = x[:, bass.ds(at, D)]
                        dve.scalar_tensor_tensor(out=xt, in0=y_ps[1 - e][:, :], scalar=0.5, in1=xt,
                                                 op0=ALU.mult, op1=ALU.add).then_inc(upd_done, 1)
                        if phase == 0:
                            tile_stats(t - 1, t + (TILES - 1), n)

                norm(0, 0)
                norm(1, 1)
                dve.wait_ge(fxh_done, base + 1)
                split_lo(fx_lo[0], xt_ps[0], fx_hi[0], fxl_done)
                step(0, 0, prev=False)
                for t in (1, 2):
                    step(t, t % 2)
                with dve.Fori(0, FLOOP) as k:
                    for e in (1, 0):
                        step(2 * k + (4 - e), e)
                    if phase == 0:
                        dequant(k)
                for t in range(TILES - 3, TILES):
                    step(t, t % 2, ahead=t < TILES - 1, two=t < TILES - 2)
                    if phase == 0:
                        dequant(t - (TILES - 3) + FLOOP)
                step(TILES, 0, here=False, ahead=False, two=False)

            dve.wait_ge(const_in, 16 * NDMA_CONST)
            for t in range(TILES):
                dve.wait_ge(xin[t // 4], 16)
                tile_stats(t, t)
            roots(0, TILES)
            ffn(0)
            barrier(dve, 1)

            roots(1, 2 * TILES)
            norm(0, 0)
            norm(1, 1)
            with dve.Fori(0, TILES // 2 - 1) as k:
                for e in range(2):
                    dve.wait_ge(xt_done, 2 * k + (TILES + e + 1))
                    norm(2 * k + (e + 2), e)
            barrier(dve, 2)

            def qk_lo(j):
                n = value(dve, j + 1)
                dve.wait_ge(kth_done, n)
                split_lo(kT_lo[:, :].rearrange("p (t k) -> p t k", t=HALVES),
                         kv_ps[:, :].rearrange("p (t k) -> p t k", t=HALVES)[:, :, 0:P],
                         kT_hi[:, :].rearrange("p (t k) -> p t k", t=HALVES), ktl_done)
                dve.wait_ge(qth_done, n)
                split_lo(qT1_lo[:, :], q_ps[1][:, :], qT1_hi[:, :], qtl_done)

            def rope(j, t):
                dve.wait_ge(q_done[t], j + 1)
                q = q_ps[t][:, :].rearrange("p (h e d) -> p h e d", h=REP, e=2)
                c = rope_c[:, t, :].rearrange("p (h d) -> p h d", d=64)
                dve.tensor_tensor(c, q_ps[t][:, :].rearrange("p (h d) -> p h d", d=64),
                                  cosq[:, t, :].unsqueeze(1).to_broadcast([P, 2 * REP, 64]), ALU.mult)
                s = rope_s[:, t, :].rearrange("p (h e d) -> p h e d", h=REP, e=2)
                dve.tensor_tensor(s, q[:, :, ::-1, :], sinq[:, t, :, :].unsqueeze(1).to_broadcast([P, REP, 2, 64]),
                                  ALU.mult).then_inc(mul_done[t], 1)

            def rope_k(j):
                dve.wait_ge(kv_done, j + 1)
                k = kv_ps[:, :].rearrange("p (t e d) -> p t e d", t=HALVES, d=64)[:, :, 0:2, :]
                dve.tensor_tensor(ropek_c[:, :, :].rearrange("p t (e d) -> p t e d", e=2), k,
                                  cosk[:, :, :].unsqueeze(2).to_broadcast([P, HALVES, 2, 64]), ALU.mult)
                dve.tensor_tensor(ropek_s[:, :, :].rearrange("p t (e d) -> p t e d", e=2), k[:, :, ::-1, :],
                                  sink[:, :, :, :], ALU.mult).then_inc(mulk_done, 1)

            def accumulate(j, t):
                dve.wait_ge(y_done[t], j + 1)
                at = value(dve, (j & (B - 1)) * (HALVES * D) + t * D)
                xt = x[:, bass.ds(at, D)]
                dve.tensor_tensor(xt, y_ps[t][:, :], xt, ALU.add).then_inc(acc_done[t], 1)

            def row_max(i, t):
                dve.wait_ge(s_done[t], i + 1)
                s = s_ps[:, 512 * t:512 * (2 * t + 1)].rearrange("p (h k) -> p h k", h=REP)
                dve.tensor_reduce(nmax[:, t, :], s, AX.X, ALU.max, negate=True).then_inc(nmax_done[t], 1)

            def item(i, first=False, last=False, prep=True):
                n = value(dve, i + 1)
                row_max(i, 0)
                row_max(i, 1)
                dve.wait_ge(vh_done, n)
                split_lo(v_lo[:, :, :], kv_ps[:, :].rearrange("p (t k) -> p t k", t=HALVES)[:, :, P:S],
                         v_hi[:, :, :], vl_done)
                dve.wait_ge(exp_done[0], n)
                dve.reciprocal(rinv[:, 0, :], rsum[:, 0, :]).then_inc(rinv_done[0], 1)
                if not last:
                    rope(i + 1, 0)
                dve.wait_ge(exp_done[1], n)
                dve.reciprocal(rinv[:, 1, :], rsum[:, 1, :]).then_inc(rinv_done[1], 1)
                if not last:
                    rope(i + 1, 1)
                    rope_k(i + 1)
                if not first:
                    accumulate(i - 1, 0)
                if prep:
                    dequant(i + AHEAD)
                for k in range(3):
                    dve.wait_ge(pth_done[k], n)
                    split_lo(pT_lo[:, k, :], s_ps[:, k * 512:(k + 1) * 512], pT_hi[:, k, :], ptl_done[k])
                if not last:
                    qk_lo(i + 1)
                if not first:
                    accumulate(i - 1, 1)
                for t in range(HALVES):
                    dve.wait_ge(oh_done[t], n)
                    split_lo(oT_lo[:, t, :], y_ps[t][:, :], oT_hi[:, t, :], ol_done[t])

            dequant(PIECES)
            rope(0, 0)
            rope(0, 1)
            rope_k(0)
            qk_lo(0)
            item(0, first=True)
            with dve.Fori(1, ITEMS - AHEAD) as i:
                item(i)
            with dve.Fori(ITEMS - AHEAD, ITEMS - 1) as i:
                item(i, prep=False)
            item(ITEMS - 1, last=True, prep=False)
            for t in range(HALVES):
                accumulate(ITEMS - 1, t)
            barrier(dve, 3)

            with dve.Fori(0, TILES) as t:
                tile_stats(t, t + 2 * TILES)
            roots(2, 3 * TILES)
            ffn(1)

        @block.gpsimd
        def _(pool):
            def weight_lo(r, at, scaled):
                pool.wait_ge(wh_done, r + 1)
                raw = value(pool, (r & 1) * PW)
                src = scales[:, bass.ds(raw, PW)] if scaled else f32(codes[:, bass.ds(raw, PW)])
                pool.tensor_tensor(w_lo[:, bass.ds(at, PW)], src, f32(w_hi[:, bass.ds(at, PW)]), ALU.subtract)\
                    .then_inc(wl_done, 1)

            def group_lo(p):
                weight_lo(p + W0, value(pool, (p & (2 * PIECES - 1)) * PW), True)

            for f in range(FPIECES):
                weight_lo(f, SLOT1 + f * PW, False)
            with pool.Fori(0, PIECES) as p:
                group_lo(p)
            barrier(pool, 1)
            barrier(pool, 2)

            def stage_lo(j):
                pool.wait_ge(xsh_done, j + 1)
                at = value(pool, (j & (B - 1)) * (DC * S))
                pool.tensor_tensor(xs_lo[:, :, :].rearrange("p c t -> p (c t)"), xT[:, bass.ds(at, DC * S)],
                                   f32(xs_hi[:, :, :].rearrange("p c t -> p (c t)")), ALU.subtract).then_inc(xsl_done, 1)

            def rope_add(j, t):
                pool.wait_ge(mul_done[t], j + 1)
                pool.tensor_tensor(rope_c[:, t, :], rope_c[:, t, :], rope_s[:, t, :], ALU.add).then_inc(rope_done[t], 1)

            def rope_add_k(j):
                pool.wait_ge(mulk_done, j + 1)
                pool.tensor_tensor(ropek_c[:, :, :], ropek_c[:, :, :], ropek_s[:, :, :], ALU.add).then_inc(ropek_done, 1)

            def normalise(i, t):
                need_apart(pool, rinv_done[t], i + 1)
                w = P * (t + 1)
                for h in range(REP):
                    at = 512 * t + h * w
                    mm = pool.tensor_scalar(probs[:, at:at + w], probs[:, at:at + w], rinv[:, t, h:h + 1], None, ALU.mult)
                mm.then_inc(norm_done[t], 1)

            def item(i, last=False, stage=True, prep=True):
                normalise(i, 0)
                if not last:
                    rope_add(i + 1, 0)
                normalise(i, 1)
                if not last:
                    rope_add(i + 1, 1)
                    rope_add_k(i + 1)
                if stage:
                    stage_lo(i + 2)
                if prep:
                    group_lo(i + AHEAD)

            stage_lo(0)
            group_lo(PIECES)
            stage_lo(1)
            rope_add(0, 0)
            rope_add(0, 1)
            rope_add_k(0)
            item(0)
            with pool.Fori(1, ITEMS - AHEAD) as i:
                item(i)
            with pool.Fori(ITEMS - AHEAD, ITEMS - 2) as i:
                item(i, prep=False)
                weight_lo(i + (F2 - ITEMS + AHEAD), SLOT0 + (i - (ITEMS - AHEAD)) * PW, False)
            item(ITEMS - 2, stage=False, prep=False)
            item(ITEMS - 1, last=True, stage=False, prep=False)
            barrier(pool, 3)


def host_arrays(i):
    n = np.asarray
    perm = np.r_[0:HD:2, 1:HD:2]
    qc, kc, vc, oc = (n(i[f"L0_attn_{k}_codes"]) for k in "qkvo")
    qs, ks, vs, os_ = (n(i[f"L0_attn_{k}_scales"]) for k in "qkvo")

    def cols(q, k, v):
        r = q.shape[0]
        q = q.reshape(r, NKV, REP, HD)[..., perm].reshape(r, NKV, QW)
        k = k.reshape(r, NKV, HD)[..., perm]
        return np.concatenate([q, k, v.reshape(r, NKV, HD)], -1)

    c = cols(qc, kc, vc).reshape(DC, P, NKV, CW).transpose(2, 1, 0, 3).reshape(NKV, P, DC * CW)
    o = oc.reshape(NKV, REP, P, D).transpose(0, 2, 1, 3).reshape(NKV, P, REP * D)
    codes = np.concatenate([c, o], -1).reshape(NKV, P, PIECES, PW).transpose(0, 2, 1, 3).reshape(ITEMS, P, PW)
    s = cols(qs, ks, vs).transpose(1, 0, 2).reshape(NKV, DC * CW)
    scales = np.concatenate([s, os_.reshape(NKV, REP * D)], -1).reshape(ITEMS, PW)

    into = np.concatenate([n(i["L0_ffn_base_W"]), n(i["L0_ffn_gate_W"]), n(i["L0_ffn_lora_A"]).reshape(ER, D)], 0).T
    f = np.zeros((P, FPIECES * PW), np.float32)
    f[:, :DC * (D + EW)] = into.reshape(DC, P, D + EW).transpose(1, 0, 2).reshape(P, -1)
    lora = n(i["L0_ffn_lora_B"]).transpose(0, 2, 1).reshape(2, KC, D)
    f[:KC, DC * (D + EW):FW] = lora.transpose(1, 0, 2).reshape(KC, 2 * D)
    f = f.reshape(P, FPIECES, PW).transpose(1, 0, 2)

    one = np.float32(1)
    inv = one / np.float32(10000.0) ** (np.arange(0, HD, 2, dtype=np.float32) / np.float32(HD))
    a = (np.arange(S, dtype=np.float32)[:, None] * inv[None, :]).reshape(HALVES, P, HD // 2).transpose(1, 0, 2)
    cos, sin = np.cos(a), np.sin(a)
    sin = np.stack([-sin, sin], 2)
    scale = np.float32(HD ** -0.5)
    neg = np.where(np.arange(P)[None, :] <= np.arange(P)[:, None], 0.0, -1e30).astype(np.float32)
    bf = mybir.dt.np(BF16)
    return {
        "x_in": n(i["L0_attn_hidden_states"]).reshape(B * S, D),
        "w_codes": codes, "w_scales": scales, "f_weights": f,
        "cos_q": cos * scale, "sin_q": sin * scale, "cos_k": cos, "sin_k": sin,
        "mask_in": np.tile(neg, (1, 4)).astype(bf), "ident_in": np.eye(P, dtype=np.float32),
        "ident16_in": np.eye(P).astype(bf), "iota_in": np.tile(np.arange(E, dtype=np.float32), (P, 1)),
    }


def kernel(**inputs):
    import concourse.bacc as bacc
    from concourse.bass_utils import run_bass_kernel_spmd

    nc = bacc.Bacc("TRN2", target_bir_lowering=False, num_devices=1, dynamic_dma_scratch_size=1024)
    arrays = {k: np.ascontiguousarray(v) for k, v in host_arrays(inputs).items()}
    args = {k: nc.dram_tensor(k, v.shape, mybir.dt.from_np(v.dtype), kind="ExternalInput").ap() for k, v in arrays.items()}
    out = nc.dram_tensor("out", (B * S, D), F32, kind="ExternalOutput").ap()
    build(nc, out=out, **args)
    r = run_bass_kernel_spmd(nc, [arrays], core_ids=[0])
    return r.results[0]["out"].reshape(B, S, D)
```

```python
from contextlib import ExitStack

import numpy as np

import concourse.bass as bass
from concourse import mybir

F32 = mybir.dt.float32
F32R = mybir.dt.float32r
BF16 = mybir.dt.bfloat16
I32 = mybir.dt.int32
U32 = mybir.dt.uint32
ALU = mybir.AluOpType
ACT = mybir.ActivationFunctionType
AX = mybir.AxisListType

P = 128
B, S, D = 8, 256, 512
TILES = B * S // P
HALVES = S // P
DC = D // P
NH, NKV, HD = 32, 8, 128
REP = NH // NKV
QW = REP * HD
CW = QW + 2 * HD
GW = DC * CW + REP * D
ITEMS = NKV * B
PIECES = B
PW = GW // PIECES
E, R = 28, 8
ER = E * R
EW = E + ER
KC = ER // 2
FW = DC * (D + EW) + 2 * D
FPIECES = -(-FW // PW)
EPS = 1e-5
PAIRS = TILES // 2
assert PAIRS == PIECES == B and HALVES == 2 and FPIECES <= B - 1
ROOTS1 = PAIRS + 2
AHEAD = B + 1
Q_AT = [c * CW for c in range(DC)]
KV_AT = [c * CW + QW for c in range(DC)]
O_AT = [DC * CW + h * D for h in range(REP)]
F_BASE = [c * (D + EW) for c in range(DC)]
F_IN = [c * (D + EW) + D for c in range(DC)]
F_LORA = [DC * (D + EW) + c * D for c in range(2)]


def build(nc, x_in, w_codes, w_scales, f_weights, cos_q, sin_q, cos_k, sin_k, mask_in, ident_in,
          ident16_in, iota_in, out):
    with ExitStack() as ctx:
        def sb(name, shape, dt=F32):
            return ctx.enter_context(nc.sbuf_tensor(name, shape, dt))

        def sem(name):
            return ctx.enter_context(nc.semaphore(name))

        x = sb("x", [P, TILES * D])
        xT = sb("xT", [P, B * DC * S])
        w_hi = sb("w_hi", [P, 2 * GW], F32R)
        w_lo = sb("w_lo", [P, 2 * GW], F32R)
        codes = sb("codes", [P, 2 * PW], I32)
        scales = sb("scales", [P, 2 * PW])
        xs_hi = sb("xs_hi", [P, DC, S], F32R)
        xs_lo = sb("xs_lo", [P, DC, S], F32R)
        probs = sb("probs", [P, 3 * 512])
        pT_hi = sb("pT_hi", [P, 3, 512], F32R)
        pT_lo = sb("pT_lo", [P, 3, 512], F32R)
        oT_hi = sb("oT_hi", [P, HALVES, 512], F32R)
        oT_lo = sb("oT_lo", [P, HALVES, 512], F32R)
        qT0 = sb("qT0", [P, 512])
        qT1_hi = sb("qT1_hi", [P, 512], F32R)
        qT1_lo = sb("qT1_lo", [P, 512], F32R)
        kT = sb("kT", [P, P])
        kT_hi = sb("kT_hi", [P, S], F32R)
        kT_lo = sb("kT_lo", [P, S], F32R)
        v_hi = sb("v_hi", [P, HALVES, HD], F32R)
        v_lo = sb("v_lo", [P, HALVES, HD], F32R)
        rope_c = sb("rope_c", [P, HALVES, QW])
        rope_s = sb("rope_s", [P, HALVES, QW])
        ropek_c = sb("ropek_c", [P, HALVES, HD])
        ropek_s = sb("ropek_s", [P, HALVES, HD])
        nmax = sb("nmax", [P, HALVES, REP])
        rsum = sb("rsum", [P, HALVES, REP])
        rinv = sb("rinv", [P, HALVES, REP])
        cosq = sb("cosq", [P, HALVES, 64])
        sinq = sb("sinq", [P, HALVES, 2, 64])
        cosk = sb("cosk", [P, HALVES, 64])
        sink = sb("sink", [P, HALVES, 2, 64])
        mask = sb("mask", [P, 4 * P], BF16)
        ident = sb("ident", [P, P])
        ident16 = sb("ident16", [P, P], BF16)
        iota = sb("iota", [P, E])
        bn = sb("bn", [P, 4, 6])
        mv = sb("mv", [P, 4, 2])
        ln_v = sb("ln_v", [P, 4])
        ln_s = sb("ln_s", [P, 4])
        ln_r = sb("ln_r", [P, 4])
        ln_t = sb("ln_t", [P, 4])
        rstd = sb("rstd", [P, 4])
        nmr = sb("nmr", [P, 4])
        logits = sb("logits", [P, 2, E])
        top = sb("top", [P, 2, 8])
        topi = sb("topi", [P, 2, 8], U32)
        topf = sb("topf", [P, 2, 2])
        gap = sb("gap", [P, 2])
        egap = sb("egap", [P, 2])
        den = sb("den", [P, 2])
        pr = sb("pr", [P, 2, 2])
        hot = sb("hot", [P, 2, 2, E])
        gate = sb("gate", [P, 2, E])
        xh = probs[:, 0:2 * D]
        xh2 = rope_s[:, :, :].rearrange("p t n -> p (t n)")
        hg = rope_c[:, :, :].rearrange("p t n -> p (t n)")[:, 0:2 * ER]
        fx_hi = pT_hi[:, 0:2, :].rearrange("p t n -> p (t n)")
        fx_lo = pT_lo[:, 0:2, :].rearrange("p t n -> p (t n)")
        hT_hi, hT_lo = oT_hi[0:KC, 0, :], oT_lo[0:KC, 0, :]

        ps = ctx.enter_context(nc.psum_tensor("ps", [P, 8 * 512], F32))
        y_all, s_ps, kv_ps = ps[:, 0:1024], ps[:, 2048:3584], ps[:, 3584:4096]
        y_ps = [ps[:, 0:512], ps[:, 512:1024]]
        q_ps = [ps[:, 1024:1536], ps[:, 1536:2048]]
        ge_ps, ht_ps = q_ps
        xt_ps, xt2_ps = ps[:, 2048:3072], ps[:, 3072:4096]

        const_in = sem("const_in")
        x_in_pair = [sem("x_in_pair0"), sem("x_in_pair1"), sem("x_in_pair2")]
        x_in_rest = sem("x_in_rest")
        f_in = [sem(f"f{f}_in") for f in range(FPIECES)]
        raw_in = sem("raw_in")
        phase_end = sem("phase_end")
        bn_done, mv_done, v_done, root_done = (sem(n) for n in ("bn_done", "mv_done", "v_done", "root_done"))
        r_done, ln1_done, ln2_done, ln3_done = (sem(n) for n in ("r_done", "ln1_done", "ln2_done", "ln3_done"))
        rstd_done, nmr_done = sem("rstd_done"), sem("nmr_done")
        xh_done, xt_done, fxh_done, fxl_done = (sem(n) for n in ("xh_done", "xt_done", "fxh_done", "fxl_done"))
        ge_done, hg_done, ht_done, hth_done, htl_done = (sem(n) for n in ("ge_done", "hg_done", "ht_done", "hth_done", "htl_done"))
        base_done, ffn_done, upd_done = sem("base_done"), sem("ffn_done"), sem("upd_done")
        xh2_done, xt2_done, xT_done = sem("xh2_done"), sem("xt2_done"), sem("xT_done")
        logit_done, top_done, topi_done, topf_done, gap_done, egap_done = (
            sem(n) for n in ("logit_done", "top_done", "topi_done", "topf_done", "gap_done", "egap_done"))
        den_done, p1_done, p2_done, hot_done, hotp_done, gate_done = (
            sem(n) for n in ("den_done", "p1_done", "p2_done", "hot_done", "hotp_done", "gate_done"))
        y_out = sem("y_out")
        w_deq, wh_done, wl_done = sem("w_deq"), sem("wh_done"), sem("wl_done")
        s_done = [sem("s0_done"), sem("s1_done")]
        q_done = [sem("q0_done"), sem("q1_done")]
        kv_done = sem("kv_done")
        pt_done = [sem(f"pt{k}_done") for k in range(3)]
        qt_done = [sem("qt0_done"), sem("qt1_done")]
        kt_done = sem("kt_done")
        o_done = [sem("o0_done"), sem("o1_done")]
        y_done = [sem("y0_done"), sem("y1_done")]
        nmax_done = [sem("nmax0_done"), sem("nmax1_done")]
        rinv_done = [sem("rinv0_done"), sem("rinv1_done")]
        mul_done = [sem("mul0_done"), sem("mul1_done")]
        mulk_done = sem("mulk_done")
        vl_done = sem("vl_done")
        ptl_done = [sem(f"ptl{k}_done") for k in range(3)]
        qtl_done, ktl_done = sem("qtl_done"), sem("ktl_done")
        ol_done = [sem("ol0_done"), sem("ol1_done")]
        acc_done = [sem("acc0_done"), sem("acc1_done")]
        exp_done = [sem("exp0_done"), sem("exp1_done")]
        vh_done, xsh_done = sem("vh_done"), sem("xsh_done")
        pth_done = [sem(f"pth{k}_done") for k in range(3)]
        qt0_copied, qth_done, kt_copied, kth_done = sem("qt0_copied"), sem("qth_done"), sem("kt_copied"), sem("kth_done")
        oh_done = [sem("oh0_done"), sem("oh1_done")]
        norm_done = [sem("norm0_done"), sem("norm1_done")]
        rope_done = [sem("rope0_done"), sem("rope1_done")]
        ropek_done = sem("ropek_done")
        xsl_done = sem("xsl_done")

        def need(eng, s, n):
            if not isinstance(n, int) or n > 0:
                eng.wait_ge(s, n)

        def value(eng, v):
            if isinstance(v, int):
                return v
            v = eng.snap(v)
            eng.to_reg(v)
            return v

        def need_apart(eng, s, n):
            n = value(eng, n)
            if not isinstance(n, int):
                eng.wait_ge(const_in, 16 * NDMA_CONST)
            need(eng, s, n)

        def barrier(eng, n):
            eng.drain().then_inc(phase_end, 1)
            eng.wait_ge(phase_end, 4 * n)

        W0, F2 = FPIECES, FPIECES + ITEMS
        SLOT1, SLOT0 = GW, 0
        NDMA_CONST = 8

        def f32(ap):
            return ap.bitcast(F32)

        block = ctx.enter_context(nc.Block())

        @block.sync
        def _(sp):
            def load_tables():
                for dst, src in ((ident, ident_in), (iota, iota_in), (cosq, cos_q), (sinq, sin_q), (cosk, cos_k),
                                 (sink, sin_k), (mask, mask_in), (ident16, ident16_in)):
                    sp.dma_start(dst[:], src).then_inc(const_in, 16)

            def load_x(p, n, done):
                sp.dma_start(x[:, p * 2 * D:(p + n) * 2 * D].rearrange("p (t d) -> p t d", d=D),
                             x_in.rearrange("(t p) d -> p t d", p=P)[:, 2 * p:2 * (p + n), :]).then_inc(done, 16)

            def room(r):
                at = value(sp, (r & 1) * PW)
                before, ins = value(sp, r - 1), value(sp, 32 * (r - W0))
                if not isinstance(r, int):
                    need_apart(sp, wl_done, before)
                need(sp, raw_in, ins)
                return at

            def ffn_piece(r, f):
                at = room(r)
                sp.dma_start(codes[:, bass.ds(at, PW)].bitcast(F32),
                             f_weights[bass.ds(f, 1)].rearrange("a p n -> (a p) n")).then_inc(raw_in, 32)

            def group_piece(r, p):
                at = room(r)
                sp.dma_start(codes[:, bass.ds(at, PW)],
                             w_codes[bass.ds(p, 1)].rearrange("a p n -> (a p) n")).then_inc(raw_in, 16)
                sp.dma_start(scales[:, bass.ds(at, PW)],
                             w_scales[bass.ds(p, 1), :].to_broadcast([P, PW])).then_inc(raw_in, 16)

            load_x(0, 1, x_in_pair[0])
            load_x(1, 1, x_in_pair[1])
            load_tables()
            for f in range(FPIECES):
                sp.dma_start(xT[:, f * PW:(f + 1) * PW], f_weights[f]).then_inc(f_in[f], 16)
            load_x(2, 1, x_in_pair[2])
            load_x(3, PAIRS - 3, x_in_rest)
            group_piece(W0, 0)
            group_piece(W0 + 1, 1)
            with sp.Fori(2, ITEMS) as p:
                group_piece(p + W0, p)
            with sp.Fori(0, FPIECES) as f:
                ffn_piece(f + F2, f)
            with sp.Fori(0, PAIRS) as p:
                need_apart(sp, upd_done, p + (PAIRS + 1))
                sp.dma_start(out[bass.ds(p * (2 * P), 2 * P), :].rearrange("(t p) d -> p t d", p=P),
                             x[:, bass.ds(p * (2 * D), 2 * D)].rearrange("p (t d) -> p t d", d=D)).then_inc(y_out, 16)
            sp.wait_ge(y_out, 16 * PAIRS)

        @block.tensor
        def _(pe):
            def split_product(ps, stationary, moving, first, last):
                (a_hi, a_lo), (b_hi, b_lo) = stationary, moving
                pe.matmul(ps, a_hi, b_hi, start=first, stop=False, skip_group_check=True)
                pe.matmul(ps, a_lo, b_hi, start=False, stop=False, skip_group_check=True)
                return pe.matmul(ps, a_hi, b_lo, start=False, stop=last, skip_group_check=True)

            def transposes(to, src, done):
                for k in range(2 * DC):
                    mm = pe.transpose(to[:, k * P:(k + 1) * P], src[:, k * P:(k + 1) * P], ident[:, :])
                mm.then_inc(done, 1)

            def tokens(t, c):
                at = (t * DC + c) * P
                return fx_hi[:, at:at + P], fx_lo[:, at:at + P]

            def weights(slot, at, w, rows=P):
                return w_hi[0:rows, slot + at:slot + at + w], w_lo[0:rows, slot + at:slot + at + w]

            def ffn_position(phase, p, slot, first=False, last=False):
                n = value(pe, p + (phase * PAIRS + 1))
                if not last:
                    pe.wait_ge(fxl_done, n)
                    for t in range(2):
                        for c in range(DC):
                            if phase == 0 and first and t == 0:
                                pe.wait_ge(wl_done, -(-(F_IN[c] + EW) // PW))
                            mm = split_product(ge_ps[:, t * EW:(t + 1) * EW], tokens(t, c),
                                               weights(slot, F_IN[c], EW), c == 0, c == DC - 1)
                    mm.then_inc(ge_done, 1)
                    if not (isinstance(p, int) and p + 1 == PAIRS):
                        pe.wait_ge(xh_done, n + 1)
                        transposes(xt_ps, xh, xt_done)
                    need(pe, upd_done, n - 1)
                    for t in range(2):
                        for c in range(DC):
                            if (t, c) == (1, DC // 2):
                                pe.wait_ge(hg_done, n)
                                for k in range(4):
                                    mm = pe.transpose(ht_ps[0:KC, k * P:(k + 1) * P], hg[:, k * KC:(k + 1) * KC], ident[:, :])
                                mm.then_inc(ht_done, 1)
                            mm = split_product(y_ps[t], tokens(t, c), weights(slot, F_BASE[c], D), c == 0, False)
                    mm.then_inc(base_done, 1)
                if phase == 0 and not first:
                    pe.wait_ge(xh2_done, p)
                    need(pe, xT_done, p - 1)
                    transposes(xt2_ps, xh2, xt2_done)
                if not last:
                    if phase == 0 and first:
                        pe.wait_ge(wl_done, FPIECES)
                    pe.wait_ge(htl_done, n)
                    for t in range(2):
                        for c in range(2):
                            at = (2 * t + c) * P
                            mm = split_product(y_ps[t], (hT_hi[:, at:at + P], hT_lo[:, at:at + P]),
                                               weights(slot, F_LORA[c], D, KC), False, c == 1)
                    mm.then_inc(ffn_done, 1)

            def ffn(phase, slot):
                pe.wait_ge(xh_done, phase * PAIRS + 1)
                transposes(xt_ps, xh, xt_done)
                ffn_position(phase, 0, slot, first=True)
                ffn_position(phase, 1, slot)
                with pe.Fori(2, PAIRS - 2) as p:
                    ffn_position(phase, p, slot)
                ffn_position(phase, PAIRS - 2, slot)
                ffn_position(phase, PAIRS - 1, slot)
                if phase == 0:
                    ffn_position(phase, PAIRS, slot, last=True)

            pe.wait_ge(const_in, 16 * NDMA_CONST)
            ffn(0, SLOT1)
            barrier(pe, 1)

            def scores(i):
                n = value(pe, i + 1)
                pe.wait_ge(qt0_copied, n)
                pe.wait_ge(kt_copied, n)
                need(pe, ptl_done[0], i)
                pe.matmul(s_ps[:, 0:512], ident16[:, :], mask[:, :], start=True, stop=False, skip_group_check=True)
                for h in range(REP):
                    mm = pe.matmul(s_ps[:, h * P:(h + 1) * P], qT0[:, h * P:(h + 1) * P], kT[:, :],
                                   start=False, stop=h == REP - 1, skip_group_check=True)
                mm.then_inc(s_done[0], 1)
                pe.wait_ge(qtl_done, n)
                pe.wait_ge(ktl_done, n)
                need(pe, ptl_done[1], i)
                need(pe, ptl_done[2], i)
                for h2 in range(REP // 2):
                    bank = s_ps[:, 512 * (1 + h2):512 * (2 + h2)].rearrange("p (h k) -> p h k", h=2)
                    pe.matmul(bank[:, :, P:S], ident16[:, :], mask[:, 0:2 * P].rearrange("p (h k) -> p h k", h=2),
                              start=True, stop=False, skip_group_check=True)
                    for h in range(2):
                        q = (2 * h2 + h) * P
                        mm = split_product(bank[:, h, :], (qT1_hi[:, q:q + P], qT1_lo[:, q:q + P]),
                                           (kT_hi[:, :], kT_lo[:, :]), False, h == 1)
                mm.then_inc(s_done[1], 1)

            def project(j):
                pe.wait_ge(xsl_done, j + 1)
                pe.wait_ge(wl_done, (j >> 3 << 3) + (W0 + PIECES) if not isinstance(j, int) else W0 + PIECES * (j // B + 1))
                slot = value(pe, ((j >> 3) & 1) * GW)
                for t in range(HALVES):
                    need(pe, (qt0_copied, qtl_done)[t], j)
                    for c in range(DC):
                        at = value(pe, slot + Q_AT[c])
                        mm = split_product(q_ps[t][:, :], [v[:, c, t * P:(t + 1) * P] for v in (xs_hi, xs_lo)],
                                           [w[:, bass.ds(at, QW)] for w in (w_hi, w_lo)], c == 0, c == DC - 1)
                    mm.then_inc(q_done[t], 1)
                    if t == 0:
                        need(pe, ktl_done, j)
                        need(pe, vl_done, j)
                    for c in range(DC):
                        at = value(pe, slot + KV_AT[c])
                        mm = split_product(kv_ps[:, t * S:(t + 1) * S],
                                           [v[:, c, t * P:(t + 1) * P] for v in (xs_hi, xs_lo)],
                                           [w[:, bass.ds(at, S)] for w in (w_hi, w_lo)], c == 0, c == DC - 1)
                mm.then_inc(kv_done, 1)

            def qk_transpose(j):
                n = value(pe, j + 1)
                for t in range(HALVES):
                    pe.wait_ge(rope_done[t], n)
                    for h in range(REP):
                        mm = pe.transpose(q_ps[t][:, h * P:(h + 1) * P], rope_c[:, t, h * P:(h + 1) * P], ident[:, :])
                    mm.then_inc(qt_done[t], 1)
                    if t == 0:
                        pe.wait_ge(ropek_done, n)
                        for u in range(HALVES):
                            mm = pe.transpose(kv_ps[:, u * S:u * S + P], ropek_c[:, u, :], ident[:, :])
                        mm.then_inc(kt_done, 1)

            def p_transpose(i):
                n = value(pe, i + 1)
                pe.wait_ge(norm_done[0], n)
                for h in range(REP):
                    mm = pe.transpose(s_ps[:, h * P:(h + 1) * P], probs[:, h * P:(h + 1) * P], ident[:, :])
                mm.then_inc(pt_done[0], 1)
                pe.wait_ge(norm_done[1], n)
                for kc in range(HALVES):
                    for h in range(REP):
                        at = 512 + h * S + kc * P
                        to = 512 * (1 + kc) + h * P
                        mm = pe.transpose(s_ps[:, to:to + P], probs[:, at:at + P], ident[:, :])
                    mm.then_inc(pt_done[1 + kc], 1)

            def values(i):
                n = value(pe, i + 1)
                pe.wait_ge(vl_done, n)
                for t in range(HALVES):
                    need(pe, acc_done[t], i)
                    for kc in range(t + 1):
                        k = (0 if t == 0 else 1 + kc)
                        pe.wait_ge(ptl_done[k], n)
                        mm = split_product(y_ps[t][:, :], (v_hi[:, kc, :], v_lo[:, kc, :]),
                                           (pT_hi[:, k, :], pT_lo[:, k, :]), kc == 0, kc == t)
                    mm.then_inc(o_done[t], 1)

            def out_project(j, t):
                pe.wait_ge(ol_done[t], j + 1)
                slot = value(pe, ((j >> 3) & 1) * GW)
                for h in range(REP):
                    at = value(pe, slot + O_AT[h])
                    mm = split_product(y_ps[t][:, :], [o[:, t, h * P:(h + 1) * P] for o in (oT_hi, oT_lo)],
                                       [w[:, bass.ds(at, D)] for w in (w_hi, w_lo)], h == 0, h == REP - 1)
                mm.then_inc(y_done[t], 1)

            def item(i, first=False, last=False):
                scores(i)
                if not last:
                    project(i + 1)
                if not first:
                    out_project(i - 1, 0)
                p_transpose(i)
                if not last:
                    qk_transpose(i + 1)
                if not first:
                    out_project(i - 1, 1)
                values(i)

            project(0)
            qk_transpose(0)
            item(0, first=True)
            with pe.Fori(1, ITEMS - 1) as i:
                item(i)
            item(ITEMS - 1, last=True)
            for t in range(HALVES):
                out_project(ITEMS - 1, t)
            barrier(pe, 2)

            pe.wait_ge(wl_done, F2 + FPIECES)
            ffn(1, SLOT0)

        @block.scalar
        def _(act):
            def split_hi(to, src, done):
                act.activation(to, src, ACT.Copy).then_inc(done, 1)

            def weight_hi(r, at, scaled):
                raw = value(act, (r & 1) * PW)
                if scaled:
                    act.wait_ge(w_deq, r - (W0 - 1))
                    src = scales[:, bass.ds(raw, PW)]
                else:
                    act.wait_ge(raw_in, 32 * (r + (1 - W0)))
                    src = f32(codes[:, bass.ds(raw, PW)])
                split_hi(w_hi[:, bass.ds(at, PW)], src, wh_done)

            def group_hi(p):
                weight_hi(p + W0, value(act, (p & (2 * PIECES - 1)) * PW), True)

            def root(c, lo, hi):
                act.wait_ge(v_done, c + 1)
                act.activation(ln_s[:, lo:hi], ln_v[:, lo:hi], ACT.Sqrt).then_inc(root_done, 1)

            def norm(p, to, col, done):
                at = value(act, p * (2 * D))
                for t in range(2):
                    mm = act.activation(to[:, t * D:(t + 1) * D], x[:, bass.ds(at + t * D, D)], ACT.Identity,
                                        bias=nmr[:, col + t:col + t + 1], scale=rstd[:, col + t:col + t + 1])
                mm.then_inc(done, 1)

            def ffn_position(phase, p, first=False, last=False):
                n = value(act, p + (phase * PAIRS + 1))
                c = p + (1 + phase * ROOTS1)
                ahead = not (isinstance(p, int) and p >= PAIRS - 2)
                behind = phase == 0 and not first
                if ahead or behind:
                    root(c, 0 if ahead else 2, 4 if behind else 2)
                if not last:
                    act.wait_ge(gap_done, n)
                    act.activation(egap[:, :], gap[:, :], ACT.Exp).then_inc(egap_done, 1)
                if ahead or behind:
                    act.wait_ge(nmr_done, c + 1)
                if ahead:
                    act.wait_ge(xt_done, n + 1)
                    norm(p + 2, xh, 0, xh_done)
                if behind:
                    norm(p - 1, xh2, 2, xh2_done)
                if not last:
                    act.wait_ge(ht_done, n)
                    split_hi(hT_hi, ht_ps[0:KC, :], hth_done)
                    if ahead or p == PAIRS - 2:
                        act.wait_ge(base_done, n)
                        split_hi(fx_hi, xt_ps, fxh_done)
                if behind:
                    act.wait_ge(xt2_done, p)
                    at = value(act, (p - 1) * (DC * S))
                    act.activation(xT[:, bass.ds(at, DC * S)].rearrange("p (c t q) -> p t c q", c=DC, t=2),
                                   xt2_ps.rearrange("p (t c q) -> p t c q", c=DC, t=2), ACT.Copy).then_inc(xT_done, 1)
                if phase == 0 and not last:
                    group_hi(p)

            def ffn(phase):
                c = phase * ROOTS1
                root(c, 0, 4)
                if phase == 0:
                    ffn_hi(0)
                act.wait_ge(nmr_done, c + 1)
                norm(0, xh, 0, xh_done)
                if phase == 0:
                    ffn_hi(1)
                act.wait_ge(xt_done, phase * PAIRS + 1)
                split_hi(fx_hi, xt_ps, fxh_done)
                if phase == 0:
                    for f in range(2, FPIECES):
                        ffn_hi(f)
                norm(1, xh, 2, xh_done)
                ffn_position(phase, 0, first=True)
                ffn_position(phase, 1)
                with act.Fori(2, PAIRS - 2) as p:
                    ffn_position(phase, p)
                ffn_position(phase, PAIRS - 2)
                ffn_position(phase, PAIRS - 1)
                if phase == 0:
                    ffn_position(phase, PAIRS, last=True)

            def ffn_hi(f):
                act.wait_ge(f_in[f], 16)
                split_hi(w_hi[:, SLOT1 + f * PW:SLOT1 + (f + 1) * PW], xT[:, f * PW:(f + 1) * PW], wh_done)

            ffn(0)
            barrier(act, 1)

            def stage_hi(j):
                need(act, kv_done, j)
                at = value(act, (j & (B - 1)) * (DC * S))
                split_hi(xs_hi[:, :, :].rearrange("p c t -> p (c t)"), xT[:, bass.ds(at, DC * S)], xsh_done)

            def qk_copies(j):
                n = value(act, j + 1)
                act.wait_ge(qt_done[0], n)
                split_hi(qT0[:, :], q_ps[0][:, :], qt0_copied)
                act.wait_ge(kt_done, n)
                split_hi(kT[:, :], kv_ps[:, 0:P], kt_copied)
                split_hi(kT_hi[:, :].rearrange("p (t k) -> p t k", t=HALVES),
                         kv_ps[:, :].rearrange("p (t k) -> p t k", t=HALVES)[:, :, 0:P], kth_done)
                act.wait_ge(qt_done[1], n)
                split_hi(qT1_hi[:, :], q_ps[1][:, :], qth_done)

            def item(i, first=False, last=False, stage=True, prep=True):
                n = value(act, i + 1)
                need(act, o_done[1], i)
                act.wait_ge(ktl_done, n)
                split_hi(v_hi[:, :, :], kv_ps[:, :].rearrange("p (t k) -> p t k", t=HALVES)[:, :, P:S], vh_done)
                for t in range(HALVES):
                    act.wait_ge(nmax_done[t], n)
                    w = P * (t + 1)
                    for h in range(REP):
                        at = 512 * t + h * w
                        mm = act.activation(probs[:, at:at + w], s_ps[:, at:at + w], ACT.Exp,
                                            bias=nmax[:, t, h:h + 1], accum_out=rsum[:, t, h:h + 1])
                    mm.then_inc(exp_done[t], 1)
                if stage:
                    stage_hi(i + 2)
                if prep:
                    group_hi(i + AHEAD)
                for k in range(3):
                    act.wait_ge(pt_done[k], n)
                    split_hi(pT_hi[:, k, :], s_ps[:, k * 512:(k + 1) * 512], pth_done[k])
                if not last:
                    qk_copies(i + 1)
                for t in range(HALVES):
                    act.wait_ge(o_done[t], n)
                    split_hi(oT_hi[:, t, :], y_ps[t][:, :], oh_done[t])

            stage_hi(0)
            group_hi(PIECES)
            stage_hi(1)
            qk_copies(0)
            item(0, first=True)
            with act.Fori(1, ITEMS - AHEAD) as i:
                item(i)
            with act.Fori(ITEMS - AHEAD, ITEMS - 2) as i:
                item(i, prep=False)
                weight_hi(i + (F2 - ITEMS + AHEAD), SLOT0 + (i - (ITEMS - AHEAD)) * PW, False)
            item(ITEMS - 2, stage=False, prep=False)
            item(ITEMS - 1, last=True, stage=False, prep=False)
            barrier(act, 2)

            ffn(1)

        @block.vector
        def _(dve):
            def stats(p, col, k):
                return dve.bn_stats(bn[:, col + k, :], x[:, bass.ds(p * (2 * D) + k * D, D)])

            def variances(c, lo, hi):
                need_apart(dve, bn_done, c + 1)
                for k in range(lo, hi):
                    mm = dve.bn_aggr(mv[:, k, :], bn[:, k, :])
                mm.then_inc(mv_done, 1)
                dve.wait_ge(mv_done, c + 1)
                dve.tensor_scalar(ln_v[:, lo:hi], mv[:, lo:hi, 1], EPS, None, ALU.add).then_inc(v_done, 1)

            def root_steps(c, lo, hi):
                m = value(dve, c + 1)
                w = slice(lo, hi)
                dve.wait_ge(root_done, m)
                dve.reciprocal(ln_r[:, w], ln_s[:, w]).then_inc(r_done, 1)
                yield
                dve.wait_ge(r_done, m)
                dve.tensor_tensor(ln_t[:, w], ln_r[:, w], ln_r[:, w], ALU.mult).then_inc(ln1_done, 1)
                yield
                dve.wait_ge(ln1_done, m)
                dve.tensor_tensor(ln_s[:, w], ln_t[:, w], ln_v[:, w], ALU.mult).then_inc(ln2_done, 1)
                yield
                dve.wait_ge(ln2_done, m)
                dve.tensor_scalar(ln_t[:, w], ln_s[:, w], -0.5, 1.5, ALU.mult, ALU.add).then_inc(ln3_done, 1)
                yield
                dve.wait_ge(ln3_done, m)
                dve.tensor_tensor(rstd[:, w], ln_r[:, w], ln_t[:, w], ALU.mult).then_inc(rstd_done, 1)
                yield
                dve.wait_ge(rstd_done, m)
                dve.scalar_tensor_tensor(out=nmr[:, w], in0=mv[:, w, 0], scalar=-1.0, in1=rstd[:, w],
                                         op0=ALU.mult, op1=ALU.mult).then_inc(nmr_done, 1)
                yield

            def split_lo(to, src, hi, done):
                dve.tensor_tensor(to, src, f32(hi), ALU.subtract).then_inc(done, 1)

            def dequant(p):
                r = p + W0
                dve.wait_ge(raw_in, 32 * p + 32)
                at = value(dve, (r & 1) * PW)
                dve.scalar_tensor_tensor(out=scales[:, bass.ds(at, PW)], in0=codes[:, bass.ds(at, PW)], scalar=-8.0,
                                         in1=scales[:, bass.ds(at, PW)], op0=ALU.add, op1=ALU.mult)\
                   .then_inc(w_deq, 1)

            def gates(m):
                dve.wait_ge(ge_done, m)
                dve.tensor_copy(logits[:, :, :], ge_ps[:, 0:2 * EW].rearrange("p (t n) -> p t n", t=2)[:, :, 0:E])\
                   .then_inc(logit_done, 1)
                need_apart(dve, logit_done, m)
                for t in range(2):
                    mm = dve.max(top[:, t, :], logits[:, t, :])
                mm.then_inc(top_done, 1)
                dve.wait_ge(top_done, m)
                dve.tensor_tensor(gap[:, :], top[:, :, 1], top[:, :, 0], ALU.subtract).then_inc(gap_done, 1)
                for t in range(2):
                    mm = dve.max_index(topi[:, t, :], top[:, t, :], logits[:, t, :])
                mm.then_inc(topi_done, 1)

            def gate_steps(m):
                dve.wait_ge(topi_done, m)
                dve.tensor_copy(topf[:, :, :], topi[:, :, 0:2]).then_inc(topf_done, 1)
                yield
                dve.wait_ge(topf_done, m)
                dve.tensor_tensor(hot[:, :, :, :].rearrange("p t k e -> p (t k) e"),
                                  iota[:, :].unsqueeze(1).to_broadcast([P, 4, E]),
                                  topf[:, :, :].rearrange("p t k -> p (t k)").unsqueeze(2).to_broadcast([P, 4, E]),
                                  ALU.is_equal).then_inc(hot_done, 1)
                yield
                dve.wait_ge(egap_done, m)
                dve.tensor_scalar(den[:, :], egap[:, :], 0.5, 0.5, ALU.mult, ALU.add).then_inc(den_done, 1)
                yield
                dve.wait_ge(den_done, m)
                dve.reciprocal(pr[:, :, 0], den[:, :]).then_inc(p1_done, 1)
                yield
                dve.wait_ge(p1_done, m)
                dve.tensor_tensor(pr[:, :, 1], pr[:, :, 0], egap[:, :], ALU.mult).then_inc(p2_done, 1)
                yield
                dve.wait_ge(hot_done, m)
                dve.wait_ge(p2_done, m)
                h = hot[:, :, :, :].rearrange("p t k e -> p (t k) e")
                dve.tensor_tensor(h, h, pr[:, :, :].rearrange("p t k -> p (t k)").unsqueeze(2).to_broadcast([P, 4, E]),
                                  ALU.mult).then_inc(hotp_done, 1)
                yield
                dve.wait_ge(hotp_done, m)
                dve.tensor_tensor(gate[:, :, :], hot[:, :, 0, :], hot[:, :, 1, :], ALU.add).then_inc(gate_done, 1)
                yield
                dve.wait_ge(gate_done, m)
                for t in range(2):
                    mm = dve.tensor_tensor(hg[:, t * ER:(t + 1) * ER].rearrange("p (e r) -> p e r", r=R),
                                           ge_ps[:, t * EW + E:(t + 1) * EW].rearrange("p (e r) -> p e r", r=R),
                                           gate[:, t, :].unsqueeze(2).to_broadcast([P, E, R]), ALU.mult)
                mm.then_inc(hg_done, 1)
                yield

            def in_turn(*chains):
                chains = list(chains)
                while chains:
                    chains = [c for c in chains if next(c, 0) != 0]

            def ffn_position(phase, p, first=False, last=False):
                n = value(dve, p + (phase * PAIRS + 1))
                c = p + (1 + phase * ROOTS1)
                ahead = not (isinstance(p, int) and p >= PAIRS - 2)
                behind = phase == 0 and not first
                lo, hi = 0 if ahead else 2, 4 if behind else 2
                if ahead:
                    for k in range(2):
                        mm = stats(p + 2, 0, k)
                if not first:
                    dve.wait_ge(ffn_done, n - 1)
                    xp = x[:, bass.ds((p - 1) * (2 * D), 2 * D)]
                    dve.scalar_tensor_tensor(out=xp, in0=y_all, scalar=0.5, in1=xp,
                                             op0=ALU.mult, op1=ALU.add).then_inc(upd_done, 1)
                if behind:
                    need_apart(dve, upd_done, n - 1)
                    for k in range(2):
                        mm = stats(p - 1, 2, k)
                chain = ahead or behind
                if chain:
                    mm.then_inc(bn_done, 1)
                    variances(c, lo, hi)
                if not last:
                    gates(n)
                in_turn(*([gate_steps(n)] * (not last) + [root_steps(c, lo, hi)] * chain))
                if not last:
                    dve.wait_ge(hth_done, n)
                    split_lo(hT_lo, ht_ps[0:KC, :], hT_hi, htl_done)
                    if ahead or p == PAIRS - 2:
                        dve.wait_ge(fxh_done, n + 1)
                        split_lo(fx_lo, xt_ps, fx_hi, fxl_done)
                if phase == 0 and not last:
                    dequant(p)

            def ffn(phase):
                c = phase * ROOTS1
                for p in range(2):
                    if phase == 0:
                        dve.wait_ge(x_in_pair[p], 16)
                    for k in range(2):
                        mm = stats(p, 2 * p, k)
                mm.then_inc(bn_done, 1)
                variances(c, 0, 4)
                for _ in root_steps(c, 0, 4):
                    pass
                if phase == 0:
                    ffn_lo(0)
                    ffn_lo(1)
                dve.wait_ge(fxh_done, phase * PAIRS + 1)
                split_lo(fx_lo, xt_ps, fx_hi, fxl_done)
                if phase == 0:
                    for f in range(2, FPIECES):
                        ffn_lo(f)
                    dve.wait_ge(x_in_pair[2], 16)
                ffn_position(phase, 0, first=True)
                if phase == 0:
                    dve.wait_ge(x_in_rest, 16)
                ffn_position(phase, 1)
                with dve.Fori(2, PAIRS - 2) as p:
                    ffn_position(phase, p)
                for p in range(PAIRS - 2, PAIRS + 1):
                    ffn_position(phase, p, last=p == PAIRS)

            def ffn_lo(f):
                dve.wait_ge(wh_done, f + 1)
                to = slice(SLOT1 + f * PW, SLOT1 + (f + 1) * PW)
                split_lo(w_lo[:, to], xT[:, f * PW:(f + 1) * PW], w_hi[:, to], wl_done)

            dve.wait_ge(const_in, 16 * NDMA_CONST)
            ffn(0)
            barrier(dve, 1)

            def qk_lo(j):
                n = value(dve, j + 1)
                dve.wait_ge(kth_done, n)
                split_lo(kT_lo[:, :].rearrange("p (t k) -> p t k", t=HALVES),
                         kv_ps[:, :].rearrange("p (t k) -> p t k", t=HALVES)[:, :, 0:P],
                         kT_hi[:, :].rearrange("p (t k) -> p t k", t=HALVES), ktl_done)
                dve.wait_ge(qth_done, n)
                split_lo(qT1_lo[:, :], q_ps[1][:, :], qT1_hi[:, :], qtl_done)

            def rope(j, t):
                dve.wait_ge(q_done[t], j + 1)
                q = q_ps[t][:, :].rearrange("p (h e d) -> p h e d", h=REP, e=2)
                c = rope_c[:, t, :].rearrange("p (h d) -> p h d", d=64)
                dve.tensor_tensor(c, q_ps[t][:, :].rearrange("p (h d) -> p h d", d=64),
                                  cosq[:, t, :].unsqueeze(1).to_broadcast([P, 2 * REP, 64]), ALU.mult)
                s = rope_s[:, t, :].rearrange("p (h e d) -> p h e d", h=REP, e=2)
                dve.tensor_tensor(s, q[:, :, ::-1, :], sinq[:, t, :, :].unsqueeze(1).to_broadcast([P, REP, 2, 64]),
                                  ALU.mult).then_inc(mul_done[t], 1)

            def rope_k(j):
                dve.wait_ge(kv_done, j + 1)
                k = kv_ps[:, :].rearrange("p (t e d) -> p t e d", t=HALVES, d=64)[:, :, 0:2, :]
                dve.tensor_tensor(ropek_c[:, :, :].rearrange("p t (e d) -> p t e d", e=2), k,
                                  cosk[:, :, :].unsqueeze(2).to_broadcast([P, HALVES, 2, 64]), ALU.mult)
                dve.tensor_tensor(ropek_s[:, :, :].rearrange("p t (e d) -> p t e d", e=2), k[:, :, ::-1, :],
                                  sink[:, :, :, :], ALU.mult).then_inc(mulk_done, 1)

            def accumulate(j, t):
                dve.wait_ge(y_done[t], j + 1)
                at = value(dve, (j & (B - 1)) * (HALVES * D) + t * D)
                xt = x[:, bass.ds(at, D)]
                dve.tensor_tensor(xt, y_ps[t][:, :], xt, ALU.add).then_inc(acc_done[t], 1)

            def row_max(i, t):
                dve.wait_ge(s_done[t], i + 1)
                s = s_ps[:, 512 * t:512 * (2 * t + 1)].rearrange("p (h k) -> p h k", h=REP)
                dve.tensor_reduce(nmax[:, t, :], s, AX.X, ALU.max, negate=True).then_inc(nmax_done[t], 1)

            def normalise(n, t):
                dve.wait_ge(exp_done[t], n)
                dve.reciprocal(rinv[:, t, :], rsum[:, t, :]).then_inc(rinv_done[t], 1)
                dve.wait_ge(rinv_done[t], n)
                w = P * (t + 1)
                for h in range(REP):
                    at = 512 * t + h * w
                    mm = dve.tensor_scalar(probs[:, at:at + w], probs[:, at:at + w], rinv[:, t, h:h + 1], None, ALU.mult)
                mm.then_inc(norm_done[t], 1)

            def item(i, first=False, last=False, prep=True):
                n = value(dve, i + 1)
                row_max(i, 0)
                row_max(i, 1)
                dve.wait_ge(vh_done, n)
                split_lo(v_lo[:, :, :], kv_ps[:, :].rearrange("p (t k) -> p t k", t=HALVES)[:, :, P:S],
                         v_hi[:, :, :], vl_done)
                normalise(n, 0)
                if not last:
                    rope(i + 1, 0)
                normalise(n, 1)
                if not last:
                    rope(i + 1, 1)
                    rope_k(i + 1)
                if not first:
                    accumulate(i - 1, 0)
                if prep:
                    dequant(i + AHEAD)
                for k in range(3):
                    dve.wait_ge(pth_done[k], n)
                    split_lo(pT_lo[:, k, :], s_ps[:, k * 512:(k + 1) * 512], pT_hi[:, k, :], ptl_done[k])
                if not first:
                    accumulate(i - 1, 1)
                if not last:
                    qk_lo(i + 1)
                for t in range(HALVES):
                    dve.wait_ge(oh_done[t], n)
                    split_lo(oT_lo[:, t, :], y_ps[t][:, :], oT_hi[:, t, :], ol_done[t])

            dequant(PIECES)
            rope(0, 0)
            rope(0, 1)
            rope_k(0)
            qk_lo(0)
            item(0, first=True)
            with dve.Fori(1, ITEMS - AHEAD) as i:
                item(i)
            with dve.Fori(ITEMS - AHEAD, ITEMS - 1) as i:
                item(i, prep=False)
            item(ITEMS - 1, last=True, prep=False)
            for t in range(HALVES):
                accumulate(ITEMS - 1, t)
            barrier(dve, 2)

            ffn(1)

        @block.gpsimd
        def _(pool):
            def weight_lo(r, at, scaled):
                pool.wait_ge(wh_done, r + 1)
                raw = value(pool, (r & 1) * PW)
                src = scales[:, bass.ds(raw, PW)] if scaled else f32(codes[:, bass.ds(raw, PW)])
                pool.tensor_tensor(w_lo[:, bass.ds(at, PW)], src, f32(w_hi[:, bass.ds(at, PW)]), ALU.subtract)\
                    .then_inc(wl_done, 1)

            def group_lo(p):
                weight_lo(p + W0, value(pool, (p & (2 * PIECES - 1)) * PW), True)

            with pool.Fori(0, PIECES) as p:
                group_lo(p)
            barrier(pool, 1)

            def stage_lo(j):
                pool.wait_ge(xsh_done, j + 1)
                at = value(pool, (j & (B - 1)) * (DC * S))
                pool.tensor_tensor(xs_lo[:, :, :].rearrange("p c t -> p (c t)"), xT[:, bass.ds(at, DC * S)],
                                   f32(xs_hi[:, :, :].rearrange("p c t -> p (c t)")), ALU.subtract).then_inc(xsl_done, 1)

            def rope_add(j, t):
                pool.wait_ge(mul_done[t], j + 1)
                pool.tensor_tensor(rope_c[:, t, :], rope_c[:, t, :], rope_s[:, t, :], ALU.add).then_inc(rope_done[t], 1)

            def rope_add_k(j):
                pool.wait_ge(mulk_done, j + 1)
                pool.tensor_tensor(ropek_c[:, :, :], ropek_c[:, :, :], ropek_s[:, :, :], ALU.add).then_inc(ropek_done, 1)

            def item(i, last=False, stage=True, prep=True):
                if not last:
                    rope_add(i + 1, 0)
                    rope_add(i + 1, 1)
                    rope_add_k(i + 1)
                if stage:
                    stage_lo(i + 2)
                if prep:
                    group_lo(i + AHEAD)

            stage_lo(0)
            group_lo(PIECES)
            stage_lo(1)
            rope_add(0, 0)
            rope_add(0, 1)
            rope_add_k(0)
            item(0)
            with pool.Fori(1, ITEMS - AHEAD) as i:
                item(i)
            with pool.Fori(ITEMS - AHEAD, ITEMS - 2) as i:
                item(i, prep=False)
                weight_lo(i + (F2 - ITEMS + AHEAD), SLOT0 + (i - (ITEMS - AHEAD)) * PW, False)
            item(ITEMS - 2, stage=False, prep=False)
            item(ITEMS - 1, last=True, stage=False, prep=False)
            barrier(pool, 2)


def host_arrays(i):
    n = np.asarray
    perm = np.r_[0:HD:2, 1:HD:2]
    qc, kc, vc, oc = (n(i[f"L0_attn_{k}_codes"]) for k in "qkvo")
    qs, ks, vs, os_ = (n(i[f"L0_attn_{k}_scales"]) for k in "qkvo")

    def cols(q, k, v):
        r = q.shape[0]
        q = q.reshape(r, NKV, REP, HD)[..., perm].reshape(r, NKV, QW)
        k = k.reshape(r, NKV, HD)[..., perm]
        return np.concatenate([q, k, v.reshape(r, NKV, HD)], -1)

    c = cols(qc, kc, vc).reshape(DC, P, NKV, CW).transpose(2, 1, 0, 3).reshape(NKV, P, DC * CW)
    o = oc.reshape(NKV, REP, P, D).transpose(0, 2, 1, 3).reshape(NKV, P, REP * D)
    codes = np.concatenate([c, o], -1).reshape(NKV, P, PIECES, PW).transpose(0, 2, 1, 3).reshape(ITEMS, P, PW)
    s = cols(qs, ks, vs).transpose(1, 0, 2).reshape(NKV, DC * CW)
    scales = np.concatenate([s, os_.reshape(NKV, REP * D)], -1).reshape(ITEMS, PW)

    into = np.concatenate([n(i["L0_ffn_base_W"]), n(i["L0_ffn_gate_W"]), n(i["L0_ffn_lora_A"]).reshape(ER, D)], 0).T
    f = np.zeros((P, FPIECES * PW), np.float32)
    f[:, :DC * (D + EW)] = into.reshape(DC, P, D + EW).transpose(1, 0, 2).reshape(P, -1)
    lora = n(i["L0_ffn_lora_B"]).transpose(0, 2, 1).reshape(2, KC, D)
    f[:KC, DC * (D + EW):FW] = lora.transpose(1, 0, 2).reshape(KC, 2 * D)
    f = f.reshape(P, FPIECES, PW).transpose(1, 0, 2)

    one = np.float32(1)
    inv = one / np.float32(10000.0) ** (np.arange(0, HD, 2, dtype=np.float32) / np.float32(HD))
    a = (np.arange(S, dtype=np.float32)[:, None] * inv[None, :]).reshape(HALVES, P, HD // 2).transpose(1, 0, 2)
    cos, sin = np.cos(a), np.sin(a)
    sin = np.stack([-sin, sin], 2)
    scale = np.float32(HD ** -0.5)
    neg = np.where(np.arange(P)[None, :] <= np.arange(P)[:, None], 0.0, -1e30).astype(np.float32)
    bf = mybir.dt.np(BF16)
    return {
        "x_in": n(i["L0_attn_hidden_states"]).reshape(B * S, D),
        "w_codes": codes, "w_scales": scales, "f_weights": f,
        "cos_q": cos * scale, "sin_q": sin * scale, "cos_k": cos, "sin_k": sin,
        "mask_in": np.tile(neg, (1, 4)).astype(bf), "ident_in": np.eye(P, dtype=np.float32),
        "ident16_in": np.eye(P).astype(bf), "iota_in": np.tile(np.arange(E, dtype=np.float32), (P, 1)),
    }


def kernel(**inputs):
    import concourse.bacc as bacc
    from concourse.bass_utils import run_bass_kernel_spmd

    nc = bacc.Bacc("TRN2", target_bir_lowering=False, num_devices=1, dynamic_dma_scratch_size=1024)
    arrays = {k: np.ascontiguousarray(v) for k, v in host_arrays(inputs).items()}
    args = {k: nc.dram_tensor(k, v.shape, mybir.dt.from_np(v.dtype), kind="ExternalInput").ap() for k, v in arrays.items()}
    out = nc.dram_tensor("out", (B * S, D), F32, kind="ExternalOutput").ap()
    build(nc, out=out, **args)
    r = run_bass_kernel_spmd(nc, [arrays], core_ids=[0])
    return r.results[0]["out"].reshape(B, S, D)
```

```python
from contextlib import ExitStack

import numpy as np

import concourse.bass as bass
from concourse import mybir

F32 = mybir.dt.float32
F32R = mybir.dt.float32r
I32 = mybir.dt.int32
U32 = mybir.dt.uint32
ALU = mybir.AluOpType
ACT = mybir.ActivationFunctionType
AX = mybir.AxisListType

P = 128
B, S, D = 8, 256, 512
TILES = B * S // P
HALVES = S // P
DC = D // P
NH, NKV, HD = 32, 8, 128
REP = NH // NKV
QW = REP * HD
CW = QW + 2 * HD
GW = DC * CW + REP * D
ITEMS = NKV * B
PIECES = B
PW = GW // PIECES
E, R = 28, 8
ER = E * R
EW = E + ER
KC = ER // 2
FW = DC * (D + EW) + 2 * D
FPIECES = -(-FW // PW)
EPS = 1e-5
PAIRS = TILES // 2
assert PAIRS == PIECES == B and HALVES == 2 and FPIECES <= B - 1
ROOTS1 = PAIRS + 3
AHEAD = B + 1
Q_AT = [c * CW for c in range(DC)]
KV_AT = [c * CW + QW for c in range(DC)]
O_AT = [DC * CW + h * D for h in range(REP)]
F_BASE = [c * (D + EW) for c in range(DC)]
F_IN = [c * (D + EW) + D for c in range(DC)]
F_LORA = [DC * (D + EW) + c * D for c in range(2)]


def build(nc, x_in, w_codes, w_scales, f_weights, cos_q, sin_q, cos_k, sin_k, mask_in, ident_in,
          iota_in, out):
    with ExitStack() as ctx:
        def sb(name, shape, dt=F32):
            return ctx.enter_context(nc.sbuf_tensor(name, shape, dt))

        def sem(name):
            return ctx.enter_context(nc.semaphore(name))

        x = sb("x", [P, TILES * D])
        xT = sb("xT", [P, B * DC * S])
        w_hi = sb("w_hi", [P, 2 * GW], F32R)
        w_lo = sb("w_lo", [P, 2 * GW], F32R)
        codes = sb("codes", [P, 2 * PW], I32)
        scales = sb("scales", [P, 2 * PW])
        xs_hi = sb("xs_hi", [P, DC, S], F32R)
        xs_lo = sb("xs_lo", [P, DC, S], F32R)
        probs = sb("probs", [P, 3 * 512])
        pT_hi = sb("pT_hi", [P, 3, 512], F32R)
        pT_lo = sb("pT_lo", [P, 3, 512], F32R)
        oT_hi = sb("oT_hi", [P, HALVES, 512], F32R)
        oT_lo = sb("oT_lo", [P, HALVES, 512], F32R)
        qT1_hi = sb("qT1_hi", [P, 512], F32R)
        qT1_lo = sb("qT1_lo", [P, 512], F32R)
        kT = sb("kT", [P, P])
        kT_hi = sb("kT_hi", [P, S], F32R)
        kT_lo = sb("kT_lo", [P, S], F32R)
        v_hi = sb("v_hi", [P, HALVES, HD], F32R)
        v_lo = sb("v_lo", [P, HALVES, HD], F32R)
        rope_c = sb("rope_c", [P, REP, S])
        rope_s = sb("rope_s", [P, REP, S])
        ropek_c = sb("ropek_c", [P, HALVES, HD])
        ropek_s = sb("ropek_s", [P, HALVES, HD])
        nmax = sb("nmax", [P, HALVES, REP])
        rsum = sb("rsum", [P, HALVES, REP])
        rinv = sb("rinv", [P, HALVES, REP])
        cosq = sb("cosq", [P, S])
        sinq = sb("sinq", [P, S])
        cosk = sb("cosk", [P, HALVES, 64])
        sink = sb("sink", [P, HALVES, 2, 64])
        mask = sb("mask", [P, P])
        ident = sb("ident", [P, P])
        iota = sb("iota", [P, E])
        bn = sb("bn", [P, 4, 6])
        mv = sb("mv", [P, 4, 2])
        ln_v = sb("ln_v", [P, 4])
        ln_s = sb("ln_s", [P, 4])
        ln_r = sb("ln_r", [P, 4])
        ln_t = sb("ln_t", [P, 4])
        rstd = sb("rstd", [P, 4])
        nmr = sb("nmr", [P, 4])
        logits = sb("logits", [P, 2, E])
        top = sb("top", [P, 2, 8])
        topi = sb("topi", [P, 2, 8], U32)
        topf = sb("topf", [P, 2, 2])
        gap = sb("gap", [P, 2])
        egap = sb("egap", [P, 2])
        den = sb("den", [P, 2])
        pr = sb("pr", [P, 2, 2])
        hot = sb("hot", [P, 2, 2, E])
        gate = sb("gate", [P, 2, E])
        xh = [probs[:, 0:2 * D], xT[:, 0:2 * D]]
        xh2 = rope_s[:, :, :].rearrange("p t n -> p (t n)")
        hg = rope_c[:, :, :].rearrange("p t n -> p (t n)")[:, 0:2 * ER]
        fx_hi = [pT_hi[:, 0:2, :].rearrange("p t n -> p (t n)"), xs_hi[:, :, :].rearrange("p c t -> p (c t)")]
        fx_lo = [pT_lo[:, 0:2, :].rearrange("p t n -> p (t n)"), xs_lo[:, :, :].rearrange("p c t -> p (c t)")]
        hT_hi, hT_lo = oT_hi[0:KC, 0, :], oT_lo[0:KC, 0, :]

        ps = ctx.enter_context(nc.psum_tensor("ps", [P, 8 * 512], F32))
        y_all, s_ps, kv_ps = ps[:, 0:1024], ps[:, 2048:3584], ps[:, 3584:4096]
        y_ps = [ps[:, 0:512], ps[:, 512:1024]]
        q_ps = [ps[:, 1024:1536], ps[:, 1536:2048]]
        ge_ps, ht_ps = q_ps
        xt_ps, xt2_ps = ps[:, 2048:3072], ps[:, 3072:4096]
        xt_first = [xt_ps, ps[:, 1024:2048]]

        first_in, const_in = sem("first_in"), sem("const_in")
        x_in_pair = [sem("x_in_pair0"), sem("x_in_pair1"), sem("x_in_pair2")]
        x_in_rest = sem("x_in_rest")
        f_in = [sem(f"f{f}_in") for f in range(FPIECES)]
        raw_in = sem("raw_in")
        bn_done, mv_done, v_done, root_done = (sem(n) for n in ("bn_done", "mv_done", "v_done", "root_done"))
        r_done, ln1_done, ln2_done, ln3_done = (sem(n) for n in ("r_done", "ln1_done", "ln2_done", "ln3_done"))
        rstd_done, nmr_done = sem("rstd_done"), sem("nmr_done")
        xh_done, xt_done, fxh_done, fxl_done = (sem(n) for n in ("xh_done", "xt_done", "fxh_done", "fxl_done"))
        ge_done, hg_done, ht_done, hth_done, htl_done = (
            sem(n) for n in ("ge_done", "hg_done", "ht_done", "hth_done", "htl_done"))
        base_done, ffn_done, upd_done = sem("base_done"), sem("ffn_done"), sem("upd_done")
        xh2_done, xt2_done, xT_done = sem("xh2_done"), sem("xt2_done"), sem("xT_done")
        logit_done, top_done, topi_done, topf_done, gap_done, egap_done = (
            sem(n) for n in ("logit_done", "top_done", "topi_done", "topf_done", "gap_done", "egap_done"))
        den_done, p1_done, p2_done, hot_done, hotp_done, gate_done = (
            sem(n) for n in ("den_done", "p1_done", "p2_done", "hot_done", "hotp_done", "gate_done"))
        y_out = sem("y_out")
        w_deq, wh_done, wl_done = sem("w_deq"), sem("wh_done"), sem("wl_done")
        s_done = [sem("s0_done"), sem("s1_done")]
        q_done = [sem("q0_done"), sem("q1_done")]
        kv_done = sem("kv_done")
        pt_done = [sem(f"pt{k}_done") for k in range(3)]
        kt_done = sem("kt_done")
        o_done = [sem("o0_done"), sem("o1_done")]
        y_done = [sem("y0_done"), sem("y1_done")]
        mask_done = [sem("mask0_done"), sem("mask1_done")]
        nmax_done = [sem("nmax0_done"), sem("nmax1_done")]
        rinv_done = [sem("rinv0_done"), sem("rinv1_done")]
        mul_done = [sem("mul0_done"), sem("mul1_done")]
        mulk_done = sem("mulk_done")
        vl_done = sem("vl_done")
        ptl_done = [sem(f"ptl{k}_done") for k in range(3)]
        qtl_done, ktl_done = sem("qtl_done"), sem("ktl_done")
        ol_done = [sem("ol0_done"), sem("ol1_done")]
        acc_done = [sem("acc0_done"), sem("acc1_done")]
        exp_done = [sem("exp0_done"), sem("exp1_done")]
        vh_done, xsh_done = sem("vh_done"), sem("xsh_done")
        pth_done = [sem(f"pth{k}_done") for k in range(3)]
        qth_done, kt_copied, kth_done = sem("qth_done"), sem("kt_copied"), sem("kth_done")
        oh_done = [sem("oh0_done"), sem("oh1_done")]
        norm_done = [sem("norm0_done"), sem("norm1_done")]
        rope_done = [sem("rope0_done"), sem("rope1_done")]
        ropek_done = sem("ropek_done")
        xsl_done = sem("xsl_done")

        def need(eng, s, n):
            if not isinstance(n, int) or n > 0:
                eng.wait_ge(s, n)

        def value(eng, v):
            if isinstance(v, int):
                return v
            v = eng.snap(v)
            eng.to_reg(v)
            return v

        def need_apart(eng, s, n):
            n = value(eng, n)
            if not isinstance(n, int):
                eng.wait_ge(first_in, 16 * NDMA_FIRST)
            need(eng, s, n)

        W0, F2 = FPIECES, FPIECES + ITEMS
        SLOT1, SLOT0 = GW, 0
        NDMA_FIRST, NDMA_CONST = 2, 5

        def f32(ap):
            return ap.bitcast(F32)

        block = ctx.enter_context(nc.Block())

        @block.sync
        def _(sp):
            def load(done, *tables):
                for to, src in tables:
                    sp.dma_start(to[:], src).then_inc(done, 16)

            def load_x(p, n, done):
                sp.dma_start(x[:, p * 2 * D:(p + n) * 2 * D].rearrange("p (t d) -> p t d", d=D),
                             x_in.rearrange("(t p) d -> p t d", p=P)[:, 2 * p:2 * (p + n), :]).then_inc(done, 16)

            def room(r):
                at = value(sp, (r & 1) * PW)
                before, ins = value(sp, r - 1), value(sp, 32 * (r - W0))
                if not isinstance(r, int):
                    need_apart(sp, wl_done, before)
                need(sp, raw_in, ins)
                return at

            def ffn_piece(r, f):
                at = room(r)
                sp.dma_start(codes[:, bass.ds(at, PW)].bitcast(F32),
                             f_weights[bass.ds(f, 1)].rearrange("a p n -> (a p) n")).then_inc(raw_in, 32)

            def group_piece(r, p):
                at = room(r)
                sp.dma_start(codes[:, bass.ds(at, PW)],
                             w_codes[bass.ds(p, 1)].rearrange("a p n -> (a p) n")).then_inc(raw_in, 16)
                sp.dma_start(scales[:, bass.ds(at, PW)],
                             w_scales[bass.ds(p, 1), :].to_broadcast([P, PW])).then_inc(raw_in, 16)

            load_x(0, 1, x_in_pair[0])
            load(first_in, (ident, ident_in), (iota, iota_in))
            load_x(1, 1, x_in_pair[1])
            for f in range(FPIECES):
                sp.dma_start(xT[:, f * PW:(f + 1) * PW], f_weights[f]).then_inc(f_in[f], 16)
            load_x(2, 1, x_in_pair[2])
            load_x(3, PAIRS - 3, x_in_rest)
            load(const_in, (cosq, cos_q), (sinq, sin_q), (cosk, cos_k), (sink, sin_k), (mask, mask_in))
            group_piece(W0, 0)
            group_piece(W0 + 1, 1)
            with sp.Fori(2, ITEMS) as p:
                group_piece(p + W0, p)
            with sp.Fori(0, FPIECES) as f:
                ffn_piece(f + F2, f)
            with sp.Fori(0, PAIRS) as p:
                need_apart(sp, upd_done, p + (PAIRS + 1))
                sp.dma_start(out[bass.ds(p * (2 * P), 2 * P), :].rearrange("(t p) d -> p t d", p=P),
                             x[:, bass.ds(p * (2 * D), 2 * D)].rearrange("p (t d) -> p t d", d=D))\
                  .then_inc(y_out, 16)
            sp.wait_ge(y_out, 16 * PAIRS)

        @block.tensor
        def _(pe):
            def split_product(ps, stationary, moving, first, last):
                (a_hi, a_lo), (b_hi, b_lo) = stationary, moving
                pe.matmul(ps, a_hi, b_hi, start=first, stop=False, skip_group_check=True)
                pe.matmul(ps, a_lo, b_hi, start=False, stop=False, skip_group_check=True)
                return pe.matmul(ps, a_hi, b_lo, start=False, stop=last, skip_group_check=True)

            def transposes(to, src, ks=range(2 * DC)):
                for k in ks:
                    mm = pe.transpose(to[:, k * P:(k + 1) * P], src[:, k * P:(k + 1) * P], ident[:, :])
                return mm

            def tokens(phase, t, c):
                at = (t * DC + c) * P
                return fx_hi[phase][:, at:at + P], fx_lo[phase][:, at:at + P]

            def weights(slot, at, w, rows=P):
                return w_hi[0:rows, slot + at:slot + at + w], w_lo[0:rows, slot + at:slot + at + w]

            def gate_lora(phase, p, slot, first=False):
                pe.wait_ge(fxl_done, p + (phase * PAIRS + 1))
                for t in range(2):
                    for c in range(DC):
                        if phase == 0 and first and t == 0:
                            pe.wait_ge(wl_done, -(-(F_IN[c] + EW) // PW))
                        mm = split_product(ge_ps[:, t * EW:(t + 1) * EW], tokens(phase, t, c),
                                           weights(slot, F_IN[c], EW), c == 0, c == DC - 1)
                mm.then_inc(ge_done, 1)

            def ffn_position(phase, p, slot, first=False):
                n = value(pe, p + (phase * PAIRS + 1))
                if phase == 1 and first:
                    pe.wait_ge(wl_done, F2 + FPIECES)
                gate_lora(phase, p, slot, first)
                ahead = not (isinstance(p, int) and p + 1 == PAIRS)
                early = DC if phase == 1 else 2 * DC
                if ahead:
                    pe.wait_ge(xh_done, n + 1)
                    mm = transposes(xt_ps, xh[phase], range(early))
                    if early == 2 * DC:
                        mm.then_inc(xt_done, 1)
                if not first:
                    pe.wait_ge(upd_done, n - 1)
                elif phase == 1:
                    pe.wait_ge(acc_done[0], ITEMS)
                    pe.wait_ge(acc_done[1], ITEMS)
                for t in range(2):
                    for c in range(DC):
                        if (t, c) == ((1, DC - 1) if phase == 0 else (1, DC // 2)):
                            pe.wait_ge(hg_done, n)
                            for k in range(4):
                                mm = pe.transpose(ht_ps[0:KC, k * P:(k + 1) * P], hg[:, k * KC:(k + 1) * KC],
                                                  ident[:, :])
                            mm.then_inc(ht_done, 1)
                        mm = split_product(y_ps[t], tokens(phase, t, c), weights(slot, F_BASE[c], D), c == 0, False)
                mm.then_inc(base_done, 1)
                if ahead and early < 2 * DC:
                    transposes(xt_ps, xh[phase], range(early, 2 * DC)).then_inc(xt_done, 1)
                if phase == 0 and not first:
                    pe.wait_ge(xh2_done, p)
                    need(pe, xT_done, p - 1)
                    transposes(xt2_ps, xh2).then_inc(xt2_done, 1)
                if phase == 0 and first:
                    pe.wait_ge(wl_done, FPIECES)
                pe.wait_ge(htl_done, n)
                for t in range(2):
                    for c in range(2):
                        at = (2 * t + c) * P
                        mm = split_product(y_ps[t], (hT_hi[:, at:at + P], hT_lo[:, at:at + P]),
                                           weights(slot, F_LORA[c], D, KC), False, c == 1)
                mm.then_inc(ffn_done, 1)

            def first_transposes(phase):
                pe.wait_ge(xh_done, phase * PAIRS + 1)
                transposes(xt_first[phase], xh[phase]).then_inc(xt_done, 1)

            def ffn(phase, slot):
                ffn_position(phase, 0, slot, first=True)
                ffn_position(phase, 1, slot)
                with pe.Fori(2, PAIRS - 2) as p:
                    ffn_position(phase, p, slot)
                ffn_position(phase, PAIRS - 2, slot)
                ffn_position(phase, PAIRS - 1, slot)

            pe.wait_ge(first_in, 16 * NDMA_FIRST)
            first_transposes(0)
            ffn(0, SLOT1)

            def scores(i, t):
                n = value(pe, i + 1)
                if t == 0:
                    pe.wait_ge(rope_done[0], n)
                    pe.wait_ge(rope_done[1], n)
                    pe.wait_ge(kt_copied, n)
                    need(pe, ptl_done[0], i)
                    for h in range(REP):
                        mm = pe.matmul(s_ps[:, h * P:(h + 1) * P], rope_c[:, h, 0:P], kT[:, :],
                                       start=True, stop=True, skip_group_check=True)
                    mm.then_inc(s_done[0], 1)
                    return
                pe.wait_ge(qtl_done, n)
                pe.wait_ge(ktl_done, n)
                need(pe, ptl_done[1], i)
                need(pe, ptl_done[2], i)
                for h in range(REP):
                    at = 512 + h * S
                    mm = split_product(s_ps[:, at:at + S], [q[:, h * P:(h + 1) * P] for q in (qT1_hi, qT1_lo)],
                                       (kT_hi[:, :], kT_lo[:, :]), True, True)
                mm.then_inc(s_done[1], 1)

            def project(j, slot):
                pe.wait_ge(xsl_done, j + 1)
                if isinstance(j, int) and j == 0:
                    pe.wait_ge(wl_done, W0 - (-DC * CW // PW))
                else:
                    pe.wait_ge(wl_done, (j >> 3 << 3) + (W0 + PIECES))
                if isinstance(j, int) and j == 0:
                    pe.wait_ge(xT_done, PAIRS - 1)
                    project_kv(j, slot)
                    project_q(j, slot)
                else:
                    project_q(j, slot)
                    project_kv(j, slot)

            def project_q(j, slot):
                for h in range(REP):
                    bank, half = h // 2, (h % 2) * S
                    if h % 2 == 0:
                        need(pe, mul_done[bank], j)
                    for c in range(DC):
                        at = slot + Q_AT[c] + h * HD
                        mm = split_product(q_ps[bank][:, half:half + S], [w[:, at:at + HD] for w in (w_hi, w_lo)],
                                           [v[:, c, :] for v in (xs_hi, xs_lo)], c == 0, c == DC - 1)
                    if h % 2:
                        mm.then_inc(q_done[bank], 1)

            def project_kv(j, slot):
                need(pe, ktl_done, j)
                need(pe, vl_done, j)
                for t in range(HALVES):
                    for c in range(DC):
                        at = slot + KV_AT[c]
                        mm = split_product(kv_ps[:, t * S:(t + 1) * S],
                                           [v[:, c, t * P:(t + 1) * P] for v in (xs_hi, xs_lo)],
                                           [w[:, at:at + S] for w in (w_hi, w_lo)], c == 0, c == DC - 1)
                mm.then_inc(kv_done, 1)

            def k_transpose(j):
                pe.wait_ge(ropek_done, j + 1)
                for u in range(HALVES):
                    mm = pe.transpose(kv_ps[:, u * S:u * S + P], ropek_c[:, u, :], ident[:, :])
                mm.then_inc(kt_done, 1)

            def p_transpose(i):
                n = value(pe, i + 1)
                pe.wait_ge(norm_done[0], n)
                for h in range(REP):
                    mm = pe.transpose(s_ps[:, h * P:(h + 1) * P], probs[:, h * P:(h + 1) * P], ident[:, :])
                mm.then_inc(pt_done[0], 1)
                pe.wait_ge(norm_done[1], n)
                for kc in range(HALVES):
                    for h in range(REP):
                        at = 512 + h * S + kc * P
                        to = 512 * (1 + kc) + h * P
                        mm = pe.transpose(s_ps[:, to:to + P], probs[:, at:at + P], ident[:, :])
                    mm.then_inc(pt_done[1 + kc], 1)

            def values(i, t):
                n = value(pe, i + 1)
                pe.wait_ge(vl_done, n)
                need(pe, acc_done[t], i)
                for kc in range(t + 1):
                    k = (0 if t == 0 else 1 + kc)
                    pe.wait_ge(ptl_done[k], n)
                    mm = split_product(y_ps[t][:, :], (v_hi[:, kc, :], v_lo[:, kc, :]),
                                       (pT_hi[:, k, :], pT_lo[:, k, :]), kc == 0, kc == t)
                mm.then_inc(o_done[t], 1)

            def out_project(j, t):
                pe.wait_ge(ol_done[t], j + 1)
                slot = value(pe, ((j >> 3) & 1) * GW)
                for h in range(REP):
                    at = value(pe, slot + O_AT[h])
                    mm = split_product(y_ps[t][:, :], [o[:, t, h * P:(h + 1) * P] for o in (oT_hi, oT_lo)],
                                       [w[:, bass.ds(at, D)] for w in (w_hi, w_lo)], h == 0, h == REP - 1)
                mm.then_inc(y_done[t], 1)

            def item(i, slot, first=False, last=False):
                if not last:
                    project(i + 1, slot)
                if not first:
                    out_project(i - 1, 0)
                p_transpose(i)
                if not last:
                    k_transpose(i + 1)
                if not first:
                    out_project(i - 1, 1)
                for t in range(HALVES):
                    values(i, t)
                    if not last:
                        scores(i + 1, t)

            pe.wait_ge(const_in, 16 * NDMA_CONST)
            project(0, SLOT0)
            pe.wait_ge(xh2_done, PAIRS)
            transposes(xt_ps, xh[0]).then_inc(xt2_done, 1)
            k_transpose(0)
            pe.wait_ge(xT_done, PAIRS)
            for t in range(HALVES):
                scores(0, t)
            item(0, SLOT0, first=True)
            with pe.Fori(1, B - 1) as i:
                item(i, SLOT0)
            with pe.Fori(0, (NKV - 2) // 2) as g2:
                with pe.Fori(B - 1, 2 * B - 1) as b:
                    item(value(pe, g2 * (2 * B) + b), SLOT1)
                with pe.Fori(2 * B - 1, 3 * B - 1) as b:
                    item(value(pe, g2 * (2 * B) + b), SLOT0)
            with pe.Fori(ITEMS - B - 1, ITEMS - 1) as i:
                item(i, SLOT1)
            item(ITEMS - 1, None, last=True)
            first_transposes(1)
            for t in range(HALVES):
                out_project(ITEMS - 1, t)
            ffn(1, SLOT0)

        @block.scalar
        def _(act):
            def split_hi(to, src, done):
                act.activation(to, src, ACT.Copy).then_inc(done, 1)

            def weight_hi(r, at, scaled):
                raw = value(act, (r & 1) * PW)
                if scaled:
                    act.wait_ge(w_deq, r - (W0 - 1))
                    src = scales[:, bass.ds(raw, PW)]
                else:
                    act.wait_ge(raw_in, 32 * (r + (1 - W0)))
                    src = f32(codes[:, bass.ds(raw, PW)])
                split_hi(w_hi[:, bass.ds(at, PW)], src, wh_done)

            def group_hi(p):
                weight_hi(p + W0, value(act, (p & (2 * PIECES - 1)) * PW), True)

            def root(c, lo, hi):
                act.wait_ge(v_done, c + 1)
                act.activation(ln_s[:, lo:hi], ln_v[:, lo:hi], ACT.Sqrt).then_inc(root_done, 1)

            def norm(p, to, col, done):
                at = value(act, p * (2 * D))
                for t in range(2):
                    mm = act.activation(to[:, t * D:(t + 1) * D], x[:, bass.ds(at + t * D, D)], ACT.Identity,
                                        bias=nmr[:, col + t:col + t + 1], scale=rstd[:, col + t:col + t + 1])
                mm.then_inc(done, 1)

            def ffn_position(phase, p, first=False, last=False):
                n = value(act, p + (phase * PAIRS + 1))
                c = p + (2, ROOTS1 + 1)[phase]
                ahead = not (isinstance(p, int) and p >= PAIRS - 2)
                behind = phase == 0 and not first
                if ahead or behind:
                    root(c, 0 if ahead else 2, 4 if behind else 2)
                if not last:
                    act.wait_ge(gap_done, n)
                    act.activation(egap[:, :], gap[:, :], ACT.Exp).then_inc(egap_done, 1)
                if ahead or behind:
                    act.wait_ge(nmr_done, c + 1)
                if behind:
                    norm(p - 1, xh[0] if last else xh2, 2, xh2_done)
                if not last:
                    act.wait_ge(ht_done, n)
                    split_hi(hT_hi, ht_ps[0:KC, :], hth_done)
                    if ahead or p == PAIRS - 2:
                        act.wait_ge(base_done, n)
                        act.wait_ge(xt_done, n + 1)
                        split_hi(fx_hi[phase], xt_ps, fxh_done)
                if ahead:
                    norm(p + 2, xh[phase], 0, xh_done)
                if behind:
                    act.wait_ge(xt2_done, p)
                    at = value(act, (p - 1) * (DC * S))
                    act.activation(xT[:, bass.ds(at, DC * S)].rearrange("p (c t q) -> p t c q", c=DC, t=2),
                                   (xt_ps if last else xt2_ps).rearrange("p (t c q) -> p t c q", c=DC, t=2),
                                   ACT.Copy).then_inc(xT_done, 1)
                if phase == 0 and not last:
                    group_hi(p)

            def ffn(phase):
                ffn_position(phase, 0, first=True)
                ffn_position(phase, 1)
                with act.Fori(2, PAIRS - 2) as p:
                    ffn_position(phase, p)
                ffn_position(phase, PAIRS - 2)
                if phase == 0:
                    act.wait_ge(xT_done, 1)
                    stage_hi(0)
                ffn_position(phase, PAIRS - 1)

            def ffn_hi(f):
                act.wait_ge(f_in[f], 16)
                split_hi(w_hi[:, SLOT1 + f * PW:SLOT1 + (f + 1) * PW], xT[:, f * PW:(f + 1) * PW], wh_done)

            def stage_hi(j):
                need(act, kv_done, j)
                need(act, q_done[1], j)
                at = value(act, (j & (B - 1)) * (DC * S))
                split_hi(xs_hi[:, :, :].rearrange("p c t -> p (c t)"), xT[:, bass.ds(at, DC * S)], xsh_done)

            root(0, 0, 2)
            act.wait_ge(nmr_done, 1)
            norm(0, xh[0], 0, xh_done)
            ffn_hi(0)
            ffn_hi(1)
            root(1, 2, 4)
            act.wait_ge(xt_done, 1)
            split_hi(fx_hi[0], xt_ps, fxh_done)
            for f in range(2, FPIECES):
                ffn_hi(f)
            act.wait_ge(nmr_done, 2)
            norm(1, xh[0], 2, xh_done)
            ffn(0)

            def k_copies(n):
                act.wait_ge(kt_done, n)
                split_hi(kT[:, :], kv_ps[:, 0:P], kt_copied)
                split_hi(kT_hi[:, :].rearrange("p (t k) -> p t k", t=HALVES),
                         kv_ps[:, :].rearrange("p (t k) -> p t k", t=HALVES)[:, :, 0:P], kth_done)

            def q_hi(n):
                act.wait_ge(rope_done[0], n)
                act.wait_ge(rope_done[1], n)
                split_hi(qT1_hi[:, :].rearrange("p (h t) -> p h t", h=REP), rope_c[:, :, P:S], qth_done)

            def item(i, first=False, last=False, stage=True, prep=True):
                n = value(act, i + 1)
                need(act, o_done[1], i)
                act.wait_ge(ktl_done, n)
                split_hi(v_hi[:, :, :], kv_ps[:, :].rearrange("p (t k) -> p t k", t=HALVES)[:, :, P:S], vh_done)
                for t in range(HALVES):
                    act.wait_ge(nmax_done[t], n)
                    w = P * (t + 1)
                    for h in range(REP):
                        at = 512 * t + h * w
                        mm = act.activation(probs[:, at:at + w], s_ps[:, at:at + w], ACT.Exp,
                                            bias=nmax[:, t, h:h + 1], accum_out=rsum[:, t, h:h + 1])
                    mm.then_inc(exp_done[t], 1)
                if stage:
                    stage_hi(i + 2)
                if last:
                    root(ROOTS1, 0, 4)
                for k in range(3):
                    act.wait_ge(pt_done[k], n)
                    split_hi(pT_hi[:, k, :], s_ps[:, k * 512:(k + 1) * 512], pth_done[k])
                if not last:
                    nj = value(act, i + 2)
                    k_copies(nj)
                    q_hi(nj)
                if prep:
                    group_hi(i + AHEAD)
                if last:
                    act.wait_ge(nmr_done, ROOTS1 + 1)
                    norm(0, xh[1], 0, xh_done)
                for t in range(HALVES):
                    act.wait_ge(o_done[t], n)
                    split_hi(oT_hi[:, t, :], y_ps[t][:, :], oh_done[t])

            ffn_position(0, PAIRS, last=True)
            k_copies(1)
            stage_hi(1)
            q_hi(1)
            group_hi(PIECES)
            item(0, first=True)
            with act.Fori(1, ITEMS - AHEAD) as i:
                item(i)
            with act.Fori(ITEMS - AHEAD, ITEMS - 2) as i:
                item(i, prep=False)
                weight_hi(i + (F2 - ITEMS + AHEAD), SLOT0 + (i - (ITEMS - AHEAD)) * PW, False)
            item(ITEMS - 2, stage=False, prep=False)
            item(ITEMS - 1, last=True, stage=False, prep=False)
            act.wait_ge(xt_done, PAIRS + 1)
            split_hi(fx_hi[1], xt_first[1], fxh_done)
            norm(1, xh[1], 2, xh_done)
            ffn(1)

        @block.vector
        def _(dve):
            def stats(p, col, k):
                return dve.bn_stats(bn[:, col + k, :], x[:, bass.ds(p * (2 * D) + k * D, D)])

            def variances(c, lo, hi):
                need_apart(dve, bn_done, c + 1)
                for k in range(lo, hi):
                    mm = dve.bn_aggr(mv[:, k, :], bn[:, k, :])
                mm.then_inc(mv_done, 1)
                dve.wait_ge(mv_done, c + 1)
                dve.tensor_scalar(ln_v[:, lo:hi], mv[:, lo:hi, 1], EPS, None, ALU.add).then_inc(v_done, 1)

            def root_steps(c, lo, hi):
                m = value(dve, c + 1)
                w = slice(lo, hi)
                dve.wait_ge(root_done, m)
                dve.reciprocal(ln_r[:, w], ln_s[:, w]).then_inc(r_done, 1)
                yield
                dve.wait_ge(r_done, m)
                dve.tensor_tensor(ln_t[:, w], ln_r[:, w], ln_r[:, w], ALU.mult).then_inc(ln1_done, 1)
                yield
                dve.wait_ge(ln1_done, m)
                dve.tensor_tensor(ln_s[:, w], ln_t[:, w], ln_v[:, w], ALU.mult).then_inc(ln2_done, 1)
                yield
                dve.wait_ge(ln2_done, m)
                dve.tensor_scalar(ln_t[:, w], ln_s[:, w], -0.5, 1.5, ALU.mult, ALU.add).then_inc(ln3_done, 1)
                yield
                dve.wait_ge(ln3_done, m)
                dve.tensor_tensor(rstd[:, w], ln_r[:, w], ln_t[:, w], ALU.mult).then_inc(rstd_done, 1)
                yield
                dve.wait_ge(rstd_done, m)
                dve.scalar_tensor_tensor(out=nmr[:, w], in0=mv[:, w, 0], scalar=-1.0, in1=rstd[:, w],
                                         op0=ALU.mult, op1=ALU.mult).then_inc(nmr_done, 1)
                yield

            def split_lo(to, src, hi, done):
                dve.tensor_tensor(to, src, f32(hi), ALU.subtract).then_inc(done, 1)

            def dequant(p):
                r = p + W0
                dve.wait_ge(raw_in, 32 * p + 32)
                at = value(dve, (r & 1) * PW)
                dve.scalar_tensor_tensor(out=scales[:, bass.ds(at, PW)], in0=codes[:, bass.ds(at, PW)], scalar=-8.0,
                                         in1=scales[:, bass.ds(at, PW)], op0=ALU.add, op1=ALU.mult)\
                   .then_inc(w_deq, 1)

            def gates(m):
                dve.wait_ge(ge_done, m)
                dve.tensor_copy(logits[:, :, :], ge_ps[:, 0:2 * EW].rearrange("p (t n) -> p t n", t=2)[:, :, 0:E])\
                   .then_inc(logit_done, 1)
                need_apart(dve, logit_done, m)
                for t in range(2):
                    mm = dve.max(top[:, t, :], logits[:, t, :])
                mm.then_inc(top_done, 1)
                dve.wait_ge(top_done, m)
                dve.tensor_tensor(gap[:, :], top[:, :, 1], top[:, :, 0], ALU.subtract).then_inc(gap_done, 1)
                for t in range(2):
                    mm = dve.max_index(topi[:, t, :], top[:, t, :], logits[:, t, :])
                mm.then_inc(topi_done, 1)

            def gate_steps(m):
                dve.wait_ge(topi_done, m)
                dve.tensor_copy(topf[:, :, :], topi[:, :, 0:2]).then_inc(topf_done, 1)
                yield
                dve.wait_ge(topf_done, m)
                dve.tensor_tensor(hot[:, :, :, :].rearrange("p t k e -> p (t k) e"),
                                  iota[:, :].unsqueeze(1).to_broadcast([P, 4, E]),
                                  topf[:, :, :].rearrange("p t k -> p (t k)").unsqueeze(2).to_broadcast([P, 4, E]),
                                  ALU.is_equal).then_inc(hot_done, 1)
                yield
                dve.wait_ge(egap_done, m)
                dve.tensor_scalar(den[:, :], egap[:, :], 0.5, 0.5, ALU.mult, ALU.add).then_inc(den_done, 1)
                yield
                dve.wait_ge(den_done, m)
                dve.reciprocal(pr[:, :, 0], den[:, :]).then_inc(p1_done, 1)
                yield
                dve.wait_ge(p1_done, m)
                dve.tensor_tensor(pr[:, :, 1], pr[:, :, 0], egap[:, :], ALU.mult).then_inc(p2_done, 1)
                yield
                dve.wait_ge(hot_done, m)
                dve.wait_ge(p2_done, m)
                h = hot[:, :, :, :].rearrange("p t k e -> p (t k) e")
                dve.tensor_tensor(h, h, pr[:, :, :].rearrange("p t k -> p (t k)").unsqueeze(2).to_broadcast([P, 4, E]),
                                  ALU.mult).then_inc(hotp_done, 1)
                yield
                dve.wait_ge(hotp_done, m)
                dve.tensor_tensor(gate[:, :, :], hot[:, :, 0, :], hot[:, :, 1, :], ALU.add).then_inc(gate_done, 1)
                yield
                dve.wait_ge(gate_done, m)
                for t in range(2):
                    mm = dve.tensor_tensor(hg[:, t * ER:(t + 1) * ER].rearrange("p (e r) -> p e r", r=R),
                                           ge_ps[:, t * EW + E:(t + 1) * EW].rearrange("p (e r) -> p e r", r=R),
                                           gate[:, t, :].unsqueeze(2).to_broadcast([P, E, R]), ALU.mult)
                mm.then_inc(hg_done, 1)
                yield

            def in_turn(*chains):
                chains = list(chains)
                while chains:
                    chains = [c for c in chains if next(c, 0) != 0]

            def ffn_position(phase, p, first=False, last=False):
                n = value(dve, p + (phase * PAIRS + 1))
                c = p + (2, ROOTS1 + 1)[phase]
                ahead = not (isinstance(p, int) and p >= PAIRS - 2)
                behind = phase == 0 and not first
                lo, hi = 0 if ahead else 2, 4 if behind else 2
                if ahead:
                    for k in range(2):
                        mm = stats(p + 2, 0, k)
                if not first:
                    dve.wait_ge(ffn_done, n - 1)
                    xp = x[:, bass.ds((p - 1) * (2 * D), 2 * D)]
                    dve.scalar_tensor_tensor(out=xp, in0=y_all, scalar=0.5, in1=xp,
                                             op0=ALU.mult, op1=ALU.add).then_inc(upd_done, 1)
                if behind:
                    need_apart(dve, upd_done, n - 1)
                    for k in range(2):
                        mm = stats(p - 1, 2, k)
                chain = ahead or behind
                if chain:
                    mm.then_inc(bn_done, 1)
                    variances(c, lo, hi)
                if not last:
                    gates(n)
                in_turn(*([gate_steps(n)] * (not last) + [root_steps(c, lo, hi)] * chain))
                if not last:
                    dve.wait_ge(hth_done, n)
                    split_lo(hT_lo, ht_ps[0:KC, :], hT_hi, htl_done)
                    if ahead or p == PAIRS - 2:
                        dve.wait_ge(fxh_done, n + 1)
                        split_lo(fx_lo[phase], xt_ps, fx_hi[phase], fxl_done)
                if phase == 0 and not last:
                    dequant(p)

            def ffn(phase):
                ffn_position(phase, 0, first=True)
                if phase == 0:
                    dve.wait_ge(x_in_rest, 16)
                ffn_position(phase, 1)
                with dve.Fori(2, PAIRS - 2) as p:
                    ffn_position(phase, p)
                for p in range(PAIRS - 2, PAIRS + 1):
                    ffn_position(phase, p, last=p == PAIRS)

            def ffn_lo(f):
                dve.wait_ge(wh_done, f + 1)
                to = slice(SLOT1 + f * PW, SLOT1 + (f + 1) * PW)
                split_lo(w_lo[:, to], xT[:, f * PW:(f + 1) * PW], w_hi[:, to], wl_done)

            for p in range(2):
                dve.wait_ge(x_in_pair[p], 16)
                for k in range(2):
                    mm = stats(p, 2 * p, k)
                mm.then_inc(bn_done, 1)
                variances(p, 2 * p, 2 * p + 2)
                if p == 0:
                    for _ in root_steps(0, 0, 2):
                        pass
            ffn_lo(0)
            ffn_lo(1)
            for _ in root_steps(1, 2, 4):
                pass
            dve.wait_ge(fxh_done, 1)
            split_lo(fx_lo[0], xt_ps, fx_hi[0], fxl_done)
            for f in range(2, FPIECES):
                ffn_lo(f)
            dve.wait_ge(first_in, 16 * NDMA_FIRST)
            dve.wait_ge(x_in_pair[2], 16)
            ffn(0)

            def qk_lo(j):
                n = value(dve, j + 1)
                dve.wait_ge(kth_done, n)
                split_lo(kT_lo[:, :].rearrange("p (t k) -> p t k", t=HALVES),
                         kv_ps[:, :].rearrange("p (t k) -> p t k", t=HALVES)[:, :, 0:P],
                         kT_hi[:, :].rearrange("p (t k) -> p t k", t=HALVES), ktl_done)
                dve.wait_ge(qth_done, n)
                split_lo(qT1_lo[:, :].rearrange("p (h t) -> p h t", h=REP), rope_c[:, :, P:S],
                         qT1_hi[:, :].rearrange("p (h t) -> p h t", h=REP), qtl_done)

            def rope(j, b):
                dve.wait_ge(q_done[b], j + 1)
                q = q_ps[b][:, :].rearrange("p (h t) -> p h t", h=2)
                half, other = slice(0, HD // 2), slice(HD // 2, HD)
                dve.tensor_tensor(rope_c[:, 2 * b:2 * b + 2, :], q, cosq[:, :].unsqueeze(1).to_broadcast([P, 2, S]),
                                  ALU.mult)
                for to, src in ((half, other), (other, half)):
                    mm = dve.tensor_tensor(rope_s[to, 2 * b:2 * b + 2, :], q[src, :, :],
                                           sinq[src, :].unsqueeze(1).to_broadcast([HD // 2, 2, S]), ALU.mult)
                mm.then_inc(mul_done[b], 1)

            def rope_k(j):
                dve.wait_ge(kv_done, j + 1)
                k = kv_ps[:, :].rearrange("p (t e d) -> p t e d", t=HALVES, d=64)[:, :, 0:2, :]
                dve.tensor_tensor(ropek_c[:, :, :].rearrange("p t (e d) -> p t e d", e=2), k,
                                  cosk[:, :, :].unsqueeze(2).to_broadcast([P, HALVES, 2, 64]), ALU.mult)
                dve.tensor_tensor(ropek_s[:, :, :].rearrange("p t (e d) -> p t e d", e=2), k[:, :, ::-1, :],
                                  sink[:, :, :, :], ALU.mult).then_inc(mulk_done, 1)

            def accumulate(j, t):
                dve.wait_ge(y_done[t], j + 1)
                at = value(dve, (j & (B - 1)) * (HALVES * D) + t * D)
                xt = x[:, bass.ds(at, D)]
                dve.tensor_tensor(xt, y_ps[t][:, :], xt, ALU.add).then_inc(acc_done[t], 1)

            def row_max(n, t):
                dve.wait_ge(s_done[t], n)
                s = s_ps[:, 512 * t:512 * (2 * t + 1)].rearrange("p (h k) -> p h k", h=REP)
                diagonal = s[:, :, P * t:P * (t + 1)]
                dve.tensor_tensor(diagonal, diagonal, mask[:, :].unsqueeze(1).to_broadcast([P, REP, P]), ALU.add)\
                   .then_inc(mask_done[t], 1)
                dve.wait_ge(mask_done[t], n)
                dve.tensor_reduce(nmax[:, t, :], s, AX.X, ALU.max, negate=True).then_inc(nmax_done[t], 1)

            def normalise(n, t):
                dve.wait_ge(exp_done[t], n)
                dve.reciprocal(rinv[:, t, :], rsum[:, t, :]).then_inc(rinv_done[t], 1)
                dve.wait_ge(rinv_done[t], n)
                w = P * (t + 1)
                for h in range(REP):
                    at = 512 * t + h * w
                    mm = dve.tensor_scalar(probs[:, at:at + w], probs[:, at:at + w], rinv[:, t, h:h + 1], None,
                                           ALU.mult)
                mm.then_inc(norm_done[t], 1)

            def out_lo(n, t):
                dve.wait_ge(oh_done[t], n)
                split_lo(oT_lo[:, t, :], y_ps[t][:, :], oT_hi[:, t, :], ol_done[t])

            def item(i, first=False, last=False, prep=True, ahead=None):
                n = value(dve, i + 1)
                row_max(n, 0)
                if not first:
                    out_lo(i, 1)
                row_max(n, 1)
                dve.wait_ge(vh_done, n)
                split_lo(v_lo[:, :, :], kv_ps[:, :].rearrange("p (t k) -> p t k", t=HALVES)[:, :, P:S],
                         v_hi[:, :, :], vl_done)
                normalise(n, 0)
                if not last:
                    rope(i + 1, 0)
                normalise(n, 1)
                if not last:
                    rope_k(i + 1)
                    rope(i + 1, 1)
                if not first:
                    accumulate(i - 1, 0)
                if last:
                    for _ in root_steps(ROOTS1, 0, 4):
                        pass
                for k in range(3):
                    dve.wait_ge(pth_done[k], n)
                    split_lo(pT_lo[:, k, :], s_ps[:, k * 512:(k + 1) * 512], pT_hi[:, k, :], ptl_done[k])
                if prep:
                    dequant(i + AHEAD)
                if ahead is not None:
                    for k in range(2):
                        mm = stats(ahead, 2 * ahead, k)
                    if ahead == 1:
                        mm.then_inc(bn_done, 1)
                        variances(ROOTS1, 0, 4)
                if not first:
                    accumulate(i - 1, 1)
                if not last:
                    qk_lo(i + 1)
                out_lo(n, 0)
                if last:
                    out_lo(n, 1)

            dequant(PIECES)
            dve.wait_ge(const_in, 16 * NDMA_CONST)
            rope_k(0)
            rope(0, 0)
            rope(0, 1)
            qk_lo(0)
            item(0, first=True)
            with dve.Fori(1, ITEMS - AHEAD) as i:
                item(i)
            with dve.Fori(ITEMS - AHEAD, ITEMS - 3) as i:
                item(i, prep=False)
            item(ITEMS - 3, prep=False, ahead=0)
            item(ITEMS - 2, prep=False, ahead=1)
            item(ITEMS - 1, last=True, prep=False)
            dve.wait_ge(fxh_done, PAIRS + 1)
            split_lo(fx_lo[1], xt_first[1], fx_hi[1], fxl_done)
            for t in range(HALVES):
                accumulate(ITEMS - 1, t)
            ffn(1)

        @block.gpsimd
        def _(pool):
            def weight_lo(r, at, scaled):
                pool.wait_ge(wh_done, r + 1)
                raw = value(pool, (r & 1) * PW)
                src = scales[:, bass.ds(raw, PW)] if scaled else f32(codes[:, bass.ds(raw, PW)])
                pool.tensor_tensor(w_lo[:, bass.ds(at, PW)], src, f32(w_hi[:, bass.ds(at, PW)]), ALU.subtract)\
                    .then_inc(wl_done, 1)

            def group_lo(p):
                weight_lo(p + W0, value(pool, (p & (2 * PIECES - 1)) * PW), True)

            def stage_lo(j):
                pool.wait_ge(xsh_done, j + 1)
                at = value(pool, (j & (B - 1)) * (DC * S))
                pool.tensor_tensor(xs_lo[:, :, :].rearrange("p c t -> p (c t)"), xT[:, bass.ds(at, DC * S)],
                                   f32(xs_hi[:, :, :].rearrange("p c t -> p (c t)")), ALU.subtract).then_inc(xsl_done, 1)

            def rope_add(j, b):
                pool.wait_ge(mul_done[b], j + 1)
                q = rope_c[:, 2 * b:2 * b + 2, :]
                pool.tensor_tensor(q, q, rope_s[:, 2 * b:2 * b + 2, :], ALU.add).then_inc(rope_done[b], 1)

            def rope_add_k(j):
                pool.wait_ge(mulk_done, j + 1)
                pool.tensor_tensor(ropek_c[:, :, :], ropek_c[:, :, :], ropek_s[:, :, :], ALU.add).then_inc(ropek_done, 1)

            def item(i, last=False, stage=True, prep=True):
                if not last:
                    rope_add(i + 1, 0)
                    rope_add_k(i + 1)
                    rope_add(i + 1, 1)
                if stage:
                    stage_lo(i + 2)
                if prep:
                    group_lo(i + AHEAD)

            with pool.Fori(0, PIECES - 1) as p:
                group_lo(p)
            stage_lo(0)
            group_lo(PIECES - 1)
            rope_add_k(0)
            rope_add(0, 0)
            rope_add(0, 1)
            stage_lo(1)
            group_lo(PIECES)
            item(0)
            with pool.Fori(1, ITEMS - AHEAD) as i:
                item(i)
            with pool.Fori(ITEMS - AHEAD, ITEMS - 2) as i:
                item(i, prep=False)
                weight_lo(i + (F2 - ITEMS + AHEAD), SLOT0 + (i - (ITEMS - AHEAD)) * PW, False)
            item(ITEMS - 2, stage=False, prep=False)
            item(ITEMS - 1, last=True, stage=False, prep=False)


def host_arrays(i):
    n = np.asarray
    perm = np.r_[0:HD:2, 1:HD:2]
    qc, kc, vc, oc = (n(i[f"L0_attn_{k}_codes"]) for k in "qkvo")
    qs, ks, vs, os_ = (n(i[f"L0_attn_{k}_scales"]) for k in "qkvo")

    def cols(q, k, v):
        r = q.shape[0]
        q = q.reshape(r, NKV, REP, HD)[..., perm].reshape(r, NKV, QW)
        k = k.reshape(r, NKV, HD)[..., perm]
        return np.concatenate([q, k, v.reshape(r, NKV, HD)], -1)

    c = cols(qc, kc, vc).reshape(DC, P, NKV, CW).transpose(2, 1, 0, 3).reshape(NKV, P, DC * CW)
    o = oc.reshape(NKV, REP, P, D).transpose(0, 2, 1, 3).reshape(NKV, P, REP * D)
    codes = np.concatenate([c, o], -1).reshape(NKV, P, PIECES, PW).transpose(0, 2, 1, 3).reshape(ITEMS, P, PW)
    s = cols(qs, ks, vs).transpose(1, 0, 2).reshape(NKV, DC * CW)
    scales = np.concatenate([s, os_.reshape(NKV, REP * D)], -1).reshape(ITEMS, PW)

    into = np.concatenate([n(i["L0_ffn_base_W"]), n(i["L0_ffn_gate_W"]), n(i["L0_ffn_lora_A"]).reshape(ER, D)], 0).T
    f = np.zeros((P, FPIECES * PW), np.float32)
    f[:, :DC * (D + EW)] = into.reshape(DC, P, D + EW).transpose(1, 0, 2).reshape(P, -1)
    lora = n(i["L0_ffn_lora_B"]).transpose(0, 2, 1).reshape(2, KC, D)
    f[:KC, DC * (D + EW):FW] = lora.transpose(1, 0, 2).reshape(KC, 2 * D)
    f = f.reshape(P, FPIECES, PW).transpose(1, 0, 2)

    one = np.float32(1)
    inv = one / np.float32(10000.0) ** (np.arange(0, HD, 2, dtype=np.float32) / np.float32(HD))
    angle = np.arange(S, dtype=np.float32)[:, None] * inv[None, :]
    a = angle.reshape(HALVES, P, HD // 2).transpose(1, 0, 2)
    cos, sin = np.cos(a), np.sin(a)
    sin = np.stack([-sin, sin], 2)
    cos_q = np.concatenate([np.cos(angle).T] * 2)
    sin_q = np.concatenate([np.sin(angle).T, -np.sin(angle).T])
    scale = np.float32(HD ** -0.5)
    neg = np.where(np.arange(P)[None, :] <= np.arange(P)[:, None], 0.0, -1e30).astype(np.float32)
    return {
        "x_in": n(i["L0_attn_hidden_states"]).reshape(B * S, D),
        "w_codes": codes, "w_scales": scales, "f_weights": f,
        "cos_q": cos_q * scale, "sin_q": sin_q * scale, "cos_k": cos, "sin_k": sin,
        "mask_in": neg, "ident_in": np.eye(P, dtype=np.float32),
        "iota_in": np.tile(np.arange(E, dtype=np.float32), (P, 1)),
    }


def kernel(**inputs):
    import concourse.bacc as bacc
    from concourse.bass_utils import run_bass_kernel_spmd

    nc = bacc.Bacc("TRN2", target_bir_lowering=False, num_devices=1, dynamic_dma_scratch_size=1024)
    arrays = {k: np.ascontiguousarray(v) for k, v in host_arrays(inputs).items()}
    args = {k: nc.dram_tensor(k, v.shape, mybir.dt.from_np(v.dtype), kind="ExternalInput").ap() for k, v in arrays.items()}
    out = nc.dram_tensor("out", (B * S, D), F32, kind="ExternalOutput").ap()
    build(nc, out=out, **args)
    r = run_bass_kernel_spmd(nc, [arrays], core_ids=[0])
    return r.results[0]["out"].reshape(B, S, D)
```
